# Optimizing a Trainium2 kernel written in Bass

```python
import numpy as np
import jax
import jax.numpy as jnp

def _softmax(x, axis=-1):
    return jax.nn.softmax(x, axis=axis)

def _gelu(x):
    return jax.nn.gelu(x, approximate=True)

def _silu(x):
    return jax.nn.silu(x)

def _sigmoid(x):
    return jax.nn.sigmoid(x)

def _layernorm(x, axis=-1, eps=1e-05):
    m = jnp.mean(x, axis=axis, keepdims=True)
    v = jnp.var(x, axis=axis, keepdims=True)
    return (x - m) / jnp.sqrt(v + eps)

def _scatter_add(tgt, idx, src, axis=0):
    return tgt.at[idx].add(src)

def _segment_sum(src, seg, n):
    return jax.ops.segment_sum(src, seg, n)
kernel_name = 'mk_adj_resnorm_d2_adj_r2_3e52ee'

def setup_inputs(seed: int=0):
    np.random.seed(seed)
    _w = jnp.asarray

    def _rec_inputs():
        import jax
        import jax.numpy as jnp
        _gk = jax.random.key(seed)
        x = -0.0005207 + 1.001 * jax.random.normal(jax.random.fold_in(_gk, 1), (64, 128, 128), jnp.float32)
        _w = (1.0 + jnp.arange(128, dtype=jnp.float32)) ** (-0.5)
        _w = _w / _w.mean()
        _pij = jnp.clip(0.125 * _w[:, None] * _w[None, :], 0.0, 1.0)
        _a = jax.random.uniform(jax.random.fold_in(_gk, 2), (64, 128, 128)) < _pij
        _a = jnp.logical_or(_a, jnp.swapaxes(_a, -1, -2))
        _a = jnp.logical_or(_a, jnp.eye(128, dtype=bool))
        _af = _a.astype(jnp.float32)
        _af = _af * jax.random.uniform(jax.random.fold_in(_gk, 3), (64, 128, 128), jnp.float32, 0.05, 1)
        adj = _af
        return (x, adj)
    x, adj = _rec_inputs()

    def _L0_gnn_setup():
        import jax, jax.numpy as jnp
        import numpy as np
        EPS = 1e-06
        key = jax.random.key(seed)
        k_x, k_a, k_w, k_b = jax.random.split(key, 4)
        B, N, Fin, Fout = (8, 1024, 128, 128)
        X = jax.random.normal(k_x, (B, N, Fin), dtype=jnp.float32)
        A = jax.random.uniform(k_a, (B, N, N), dtype=jnp.float32)
        bound = 1.0 / np.sqrt(Fin)
        W = jax.random.uniform(k_w, (Fout, Fin), minval=-bound, maxval=bound, dtype=jnp.float32)
        b = jax.random.uniform(k_b, (Fout,), minval=-bound, maxval=bound, dtype=jnp.float32)
        return {'X': X, 'A': A, 'W': W, 'b': b}
    _L0_gnn_all = _L0_gnn_setup()
    _L0_gnn_in = {k: v for k, v in _L0_gnn_all.items() if k in ('W', 'b')}
    del _L0_gnn_all

    def _L1_gnn_setup():
        import jax, jax.numpy as jnp
        import numpy as np
        B, S, H, HID = (1, 512, 128, 128)
        LN_EPS = 1e-05

        def _layernorm(y, gamma, beta):
            mu = jnp.mean(y, axis=-1, keepdims=True)
            var = jnp.mean(jnp.square(y - mu), axis=-1, keepdims=True)
            return (y - mu) * jax.lax.rsqrt(var + LN_EPS) * gamma + beta
        key = jax.random.key(seed)
        ks = jax.random.split(key, 8)
        x = jax.random.normal(ks[0], (B, S, H), dtype=jnp.float32)
        adj = jax.random.uniform(ks[1], (B, S, S), dtype=jnp.float32)
        W1 = jax.random.normal(ks[2], (2 * H, HID), dtype=jnp.float32) / np.sqrt(2 * H)
        b1 = jnp.zeros((HID,), dtype=jnp.float32)
        W2 = jax.random.normal(ks[3], (HID, HID), dtype=jnp.float32) / np.sqrt(HID)
        b2 = jnp.zeros((HID,), dtype=jnp.float32)
        gamma = jnp.ones((HID,), dtype=jnp.float32)
        beta = jnp.zeros((HID,), dtype=jnp.float32)
        return {'x': x, 'adj': adj, 'W1': W1, 'b1': b1, 'W2': W2, 'b2': b2, 'gamma': gamma, 'beta': beta}
    _L1_gnn_all = _L1_gnn_setup()
    _L1_gnn_in = {k: v for k, v in _L1_gnn_all.items() if k in ('W1', 'b1', 'W2', 'b2', 'gamma', 'beta')}
    del _L1_gnn_all
    return {'x': x, 'adj': adj, 'L0_gnn_W': _L0_gnn_in['W'], 'L0_gnn_b': _L0_gnn_in['b'], 'L1_gnn_W1': _L1_gnn_in['W1'], 'L1_gnn_b1': _L1_gnn_in['b1'], 'L1_gnn_W2': _L1_gnn_in['W2'], 'L1_gnn_b2': _L1_gnn_in['b2'], 'L1_gnn_gamma': _L1_gnn_in['gamma'], 'L1_gnn_beta': _L1_gnn_in['beta']}

def reference(x, adj, L0_gnn_W, L0_gnn_b, L1_gnn_W1, L1_gnn_b1, L1_gnn_W2, L1_gnn_b2, L1_gnn_gamma, L1_gnn_beta):
    import jax
    import jax.numpy as jnp

    def _L0_gnn_ref(X, A, W, b):
        import jax, jax.numpy as jnp
        import numpy as np
        EPS = 1e-06
        N = A.shape[-1]
        A_hat = A + jnp.eye(N, dtype=A.dtype)
        d_inv_sqrt = (jnp.sum(A_hat, axis=-1) + EPS) ** (-0.5)
        A_norm = d_inv_sqrt[:, :, None] * A_hat * d_inv_sqrt[:, None, :]
        support = jnp.einsum('bnm,bmf->bnf', A_norm, X)
        out = jnp.einsum('bnf,of->bno', support, W) + b
        return jax.nn.relu(out)

    def _L1_gnn_ref(x, adj, W1, b1, W2, b2, gamma, beta):
        import jax, jax.numpy as jnp
        import numpy as np
        B, S, H, HID = (1, 512, 128, 128)
        LN_EPS = 1e-05

        def _layernorm(y, gamma, beta):
            mu = jnp.mean(y, axis=-1, keepdims=True)
            var = jnp.mean(jnp.square(y - mu), axis=-1, keepdims=True)
            return (y - mu) * jax.lax.rsqrt(var + LN_EPS) * gamma + beta
        hi = jnp.einsum('bsh,hk->bsk', x, W1[:H])
        hj = jnp.einsum('bsh,hk->bsk', x, W1[H:])
        h = jax.nn.relu(hi[:, :, None, :] + hj[:, None, :, :] + b1)
        y = jnp.einsum('bijk,kl->bijl', h, W2) + b2
        y = _layernorm(y, gamma, beta)
        out = jnp.einsum('bij,bijh->bih', adj, y)
        return out
    x = _layernorm(x + _L0_gnn_ref(x, adj, L0_gnn_W, L0_gnn_b), axis=-1)
    x = _layernorm(x + _L1_gnn_ref(x, adj, L1_gnn_W1, L1_gnn_b1, L1_gnn_W2, L1_gnn_b2, L1_gnn_gamma, L1_gnn_beta), axis=-1)
    return x

_drawn_inputs = setup_inputs


def setup_inputs(seed=0):
    import zlib

    import numpy as np

    out = dict(_drawn_inputs(seed))
    spreads = {'L1_gnn_b1': (0.0, 0.1),
     'L1_gnn_b2': (0.0, 0.1),
     'L1_gnn_gamma': (1.0, 0.2),
     'L1_gnn_beta': (0.0, 0.1)}
    factors = {}
    for name, (base, spread) in spreads.items():
        noise = np.random.default_rng([zlib.crc32(name.encode()), seed]).standard_normal(out[name].shape)
        drawn = base * np.exp(spread * noise) if base else spread * noise
        out[name] = jnp.asarray(drawn.astype(out[name].dtype))
    for name, factor in factors.items():
        out[name] = (out[name] * factor).astype(out[name].dtype)
    return out
```

```python
import concourse.bass as bass
from concourse import mybir
from contextlib import ExitStack


def gnn_two_layer_kernel(nc: bass.Bass, x, adj, adj_t, w0_t, b0, w1, b1, w2, b2, gamma, beta, ident_in, diag4_in, out):
    fp32 = mybir.dt.float32
    ALU = mybir.AluOpType
    ACT = mybir.ActivationFunctionType
    ds = bass.ds

    BATCH, N, F = x.shape
    HID = w2.shape[1]
    UNITS = 4
    GROUPS = N // UNITS
    COLG = 4
    STEPS = GROUPS // COLG
    HALF = GROUPS // 2
    LEAD = 3
    HRING = 4
    PRING = 3
    BANK = 512
    WX = HID + 1
    ZW = 32
    ZP = ZW - UNITS
    EPS = 1e-5
    SLOTS = BATCH + 2

    ctx = ExitStack()
    with ctx:
        def sb(name, shape, dt=fp32):
            return ctx.enter_context(nc.sbuf_tensor(name, shape, dt))

        def pb(name, shape):
            return ctx.enter_context(nc.psum_tensor(name, shape, fp32))

        def sem(name):
            return ctx.enter_context(nc.semaphore(name))

        nodes = sb("nodes", [N, SLOTS, F])
        adjn = sb("adjn", [N, SLOTS, N])
        adjt = sb("adjt", [N, SLOTS, N])
        rsum = sb("rsum", [N, SLOTS])
        ident = sb("ident", [128, 128])
        diag4 = sb("diag4", [128, UNITS])
        w0t = sb("w0t", [F, F])
        w1a = sb("w1a", [F, HID])
        w1b = sb("w1b", [F, HID])
        b1c = sb("b1c", [HID, 1])
        w2raw = sb("w2raw", [HID, HID])
        w2x = sb("w2x", [HID, WX])
        b0r = sb("b0r", [N, F])
        b2raw = sb("b2raw", [N, HID])
        b2c = sb("b2c", [N, HID])
        gammar = sb("gammar", [N, HID])
        betar = sb("betar", [N, HID])
        neghalf = sb("neghalf", [N, 1])
        selfeps = sb("selfeps", [N, 1])
        junk = sb("junk", [HID, HID])
        sums = sb("sums", [HID, 4])
        deg = sb("deg", [N, 2])
        xs = sb("xs", [N, F])
        ahat_t = sb("ahat_t", [N, N])
        supp_t = sb("supp_t", [F, N])
        l0 = sb("l0", [N, 2, F])
        l0st = sb("l0st", [N, 6])
        l0mv = sb("l0mv", [N, 2])
        l0rs = sb("l0rs", [N, 2])
        x1s = sb("x1s", [N, F])
        x1t = sb("x1t", [F, N])
        u = sb("u", [HID, N])
        v = sb("v", [HID, N])
        h = sb("h", [HID, HRING, UNITS, N])
        a = sb("a", [N, GROUPS, UNITS * WX])
        st = sb("st", [N, N, 3])
        sq = sb("sq", [N, 2, HALF, UNITS])
        sd = sb("sd", [N, 2, HALF, UNITS])
        r0 = sb("r0", [N, 2, HALF, UNITS])
        nw = sb("nw", [N, 4, HALF * UNITS])
        z = sb("z", [N, ZP + ZW * GROUPS])
        wn = sb("wn", [N, N])
        sb2 = sb("sb2", [N, HID])
        acc = sb("acc", [N, UNITS, HID])
        ep = sb("ep", [N, 4, HID])
        epst = sb("epst", [N, 6])
        epmv = sb("epmv", [N, 2])
        eprs = sb("eprs", [N, 2])

        ring = pb("ring", [128, PRING, 2, BANK])
        contr = pb("contr", [128, UNITS, HID])
        misc = pb("misc", [128, 4, 128])

        h_dve = sem("h_dve")
        h_act = sem("h_act")
        a_made = sem("a_made")
        a_stat = sem("a_stat")
        a_moved = sem("a_moved")
        sq_ready = sem("sq_ready")
        sd_ready = sem("sd_ready")
        r0_ready = sem("r0_ready")
        newton = sem("newton")
        wn_ready = sem("wn_ready")
        w_ready = sem("w_ready")
        contracted = sem("contracted")
        loaded = sem("loaded")
        x1_kept = sem("x1_kept")
        rsum_ready = sem("rsum_ready")
        deg_ready = sem("deg_ready")
        dis_ready = sem("dis_ready")
        xs_ready = sem("xs_ready")
        ahat_ready = sem("ahat_ready")
        supp_made = sem("supp_made")
        supp_moved = sem("supp_moved")
        lin_made = sem("lin_made")
        lin_scaled = sem("lin_scaled")
        res_ready = sem("res_ready")
        l0_stats = sem("l0_stats")
        l0_aggr = sem("l0_aggr")
        l0_var = sem("l0_var")
        l0_rstd = sem("l0_rstd")
        x1_ready = sem("x1_ready")
        x1t_made = sem("x1t_made")
        x1t_moved = sem("x1t_moved")
        uv_made = sem("uv_made")
        u_moved = sem("u_moved")
        uv_moved = sem("uv_moved")
        sb2_made = sem("sb2_made")
        sb2_moved = sem("sb2_moved")
        picking = sem("picking")
        contr_free = sem("contr_free")
        ep_beta = sem("ep_beta")
        ep_gamma = sem("ep_gamma")
        ep_x1 = sem("ep_x1")
        ep_sum = sem("ep_sum")
        ep_stats = sem("ep_stats")
        ep_aggr = sem("ep_aggr")
        ep_var = sem("ep_var")
        ep_rstd = sem("ep_rstd")
        ep_centred = sem("ep_centred")
        ep_done = sem("ep_done")
        consts = sem("consts")
        b2s = sem("b2s")
        w2s = sem("w2s")
        filled = sem("filled")
        stored = sem("stored")
        N_CONST = 11 * 16
        N_FILLED = 13

        block = ctx.enter_context(nc.Block())

        def node(g, e):
            return 32 * (g % COLG) + UNITS * (g // COLG) + e

        def wait_apart(eng, semaphore, value):
            value = value if isinstance(value, int) else eng.snap(eng.to_reg(value))
            eng.wait_ge(filled, N_FILLED)
            eng.wait_ge(semaphore, value)

        def step_at(g):
            k = g // COLG
            return ((k + 2), True) if k < STEPS - 2 else (k - (STEPS - 2), False)

        @block.sync
        def _(sy):
            for dst, src in ((w0t[:, :], w0_t), (ident[:, :], ident_in), (w1a[:, :], w1[0:F, :]),
                             (w1b[:, :], w1[F:2 * F, :]), (w2raw[:, :], w2), (diag4[:, :], diag4_in),
                             (b1c[:, :], b1.unsqueeze(1)),
                             (b0r[:, :], b0.unsqueeze(0).broadcast_to([N, F])),
                             (b2raw[:, :], b2.unsqueeze(0).broadcast_to([N, HID])),
                             (gammar[:, :], gamma.unsqueeze(0).broadcast_to([N, HID])),
                             (betar[:, :], beta.unsqueeze(0).broadcast_to([N, HID]))):
                sy.dma_start(dst, src).then_inc(consts, 16)
            sy.sem_inc(loaded, 48)
            with sy.Fori(1, BATCH + 1) as s:
                sy.wait_ge(loaded, s * 48)
                sy.dma_start(nodes[:, ds(s, 1), :], x[ds(s - 1, 1), :, :].rearrange("b n f -> n b f")).then_inc(loaded, 16)
                sy.dma_start(adjn[:, ds(s, 1), :], adj[ds(s - 1, 1), :, :].rearrange("b n f -> n b f")).then_inc(loaded, 16)
                sy.dma_start(adjt[:, ds(s, 1), :], adj_t[ds(s - 1, 1), :, :].rearrange("b n f -> n b f")).then_inc(loaded, 16)
            sy.wait_ge(loaded, (BATCH + 1) * 48)
            sy.sem_inc(loaded, 48)
            with sy.Fori(1, BATCH + 1) as s:
                sy.wait_ge(ep_done, s + 1)
                sy.dma_start(out[ds(s - 1, 1), :, :].rearrange("b n f -> n b f"), adjn[:, ds(s, 1), :]).then_inc(stored, 16)
            sy.wait_ge(stored, 16 * BATCH)

        @block.gpsimd
        def _(gp):
            for s in (0, SLOTS - 1):
                gp.memset(nodes[:, s, :], 0.0).then_inc(filled, 1)
                gp.memset(adjn[:, s, :], 0.0).then_inc(filled, 1)
                gp.memset(adjt[:, s, :], 0.0).then_inc(filled, 1)
            gp.memset(rsum[:, 0:1], 0.0).then_inc(filled, 1)
            gp.memset(neghalf[:, :], -0.5).then_inc(filled, 1)
            gp.memset(selfeps[:, :], 1.0 + 1e-6).then_inc(filled, 1)
            gp.memset(z[:, :], 0.0).then_inc(filled, 1)
            gp.memset(wn[:, :], 0.0).then_inc(filled, 1)
            gp.memset(a[:, :, :], 0.0).then_inc(filled, 1)
            gp.memset(st[:, :, :], 0.0).then_inc(filled, 1)
            gp.sem_inc(w_ready, 1)
            gp.sem_inc(sq_ready, 1)
            gp.sem_inc(x1_kept, 1)
            gp.sem_inc(wn_ready, 1)
            gp.sem_inc(newton, 5)
            gp.wait_ge(filled, N_FILLED)

            def degree(s):
                gp.wait_ge(rsum_ready, s)
                gp.tensor_tensor(deg[:, 0:1], rsum[:, ds(s, 1)], selfeps[:, :], ALU.add).then_inc(deg_ready, 1)
                gp.wait_ge(deg_ready, s)
                gp.tensor_tensor(deg[:, 1:2], deg[:, 0:1], neghalf[:, :], ALU.pow).then_inc(dis_ready, 1)
                gp.tensor_tensor(ahat_t[:, :].unsqueeze(1), adjt[:, ds(s, 1), :], ident[:, :].unsqueeze(1), ALU.add).then_inc(ahat_ready, 1)

            def l0_scale(s):
                wait_apart(gp, l0_aggr, s)
                gp.tensor_scalar(l0rs[:, 0:1], l0mv[:, 1:2], EPS, None, ALU.add).then_inc(l0_var, 1)
                gp.wait_ge(l0_var, s)
                gp.tensor_tensor(l0rs[:, 1:2], l0rs[:, 0:1], neghalf[:, :], ALU.pow).then_inc(l0_rstd, 1)
                wait_apart(gp, x1_ready, s)
                gp.tensor_copy(nodes[:, ds(s, 1), :], x1s[:, :].unsqueeze(1)).then_inc(x1_kept, 1)

            def gather_sq(s, half, moved):
                gp.wait_ge(a_moved, moved)
                n0 = half * HALF * UNITS
                gp.tensor_tensor(sq[:, half, :, :], st[:, n0:n0 + HALF * UNITS, 2].rearrange("p (g e) -> p g e", e=UNITS),
                                 a[:, half * HALF:(half + 1) * HALF, :].rearrange("p g (e w) -> p g e w", w=WX)[:, :, :, HID],
                                 ALU.add).then_inc(sq_ready, 1)

            def weights(s, half, count):
                flat = lambda t: t[:, half, :, :].rearrange("p g e -> p (g e)")
                k = (count - 1) * 5
                wait_apart(gp, sq_ready, count)
                gp.tensor_scalar(nw[:, 0, :], flat(sq), 1.0 / HID, sums[:, 3:4], ALU.mult, ALU.add).then_inc(newton, 1)
                gp.wait_ge(r0_ready, count)
                gp.tensor_tensor(nw[:, 1, :], flat(r0), flat(r0), ALU.mult).then_inc(newton, 1)
                gp.wait_ge(newton, k + 2)
                gp.tensor_tensor(nw[:, 2, :], nw[:, 0, :], nw[:, 1, :], ALU.mult).then_inc(newton, 1)
                wait_apart(gp, newton, k + 3)
                gp.tensor_scalar(nw[:, 3, :], nw[:, 2, :], -0.5, 1.5, ALU.mult, ALU.add).then_inc(newton, 1)
                gp.wait_ge(newton, k + 4)
                gp.tensor_tensor(nw[:, 1, :], nw[:, 3, :], flat(r0), ALU.mult).then_inc(newton, 1)
                gp.wait_ge(newton, k + 5)
                C = HALF // COLG
                at = half * C * UNITS
                adj_v = adjt[:, ds(s, 1), :].rearrange("p o (q r) -> p (o q) r", q=COLG)[:, :, at:at + C * UNITS]
                w_v = wn[:, :].rearrange("p (q r) -> p q r", q=COLG)[:, :, at:at + C * UNITS]
                gp.tensor_tensor(w_v.rearrange("p q (c e) -> p q c e", e=UNITS), adj_v.rearrange("p q (c e) -> p q c e", e=UNITS),
                                 nw[:, 1, :].rearrange("p (c q e) -> p q c e", q=COLG, e=UNITS), ALU.mult).then_inc(wn_ready, 1)
                wait_apart(gp, wn_ready, count)
                z_v = z[:, ZW * half * HALF:ZW * (half + 1) * HALF].rearrange("p (c q r) -> p c q r", q=COLG, r=ZW)[:, :, :, ZP:ZW]
                gp.tensor_copy(z_v, w_v.rearrange("p q (c e) -> p c q e", e=UNITS)).then_inc(w_ready, 1)

            def combine(s):
                gp.tensor_tensor(ep[:, 0, :], betar[:, :], rsum[:, ds(s, 1)].broadcast_to([N, HID]), ALU.mult).then_inc(ep_beta, 1)
                gp.wait_ge(contr_free, s + 1)
                gp.tensor_tensor(ep[:, 1, :], acc[:, UNITS - 1, :], gammar[:, :], ALU.mult).then_inc(ep_gamma, 1)
                gp.wait_ge(ep_gamma, s + 1)
                gp.wait_ge(ep_beta, s + 1)
                gp.wait_ge(x1_kept, s + 1)
                gp.tensor_tensor(ep[:, 2:3, :], ep[:, 1:2, :], nodes[:, ds(s, 1), :], ALU.add).then_inc(ep_x1, 1)
                gp.wait_ge(ep_x1, s + 1)
                gp.tensor_tensor(ep[:, 3, :], ep[:, 2, :], ep[:, 0, :], ALU.add).then_inc(ep_sum, 1)

            def finish(s):
                wait_apart(gp, ep_aggr, s + 1)
                gp.tensor_scalar(eprs[:, 0:1], epmv[:, 1:2], EPS, None, ALU.add).then_inc(ep_var, 1)
                gp.wait_ge(ep_var, s + 1)
                gp.tensor_tensor(eprs[:, 1:2], eprs[:, 0:1], neghalf[:, :], ALU.pow).then_inc(ep_rstd, 1)
                gp.tensor_tensor(ep[:, 2, :], ep[:, 3, :], epmv[:, 0:1].broadcast_to([N, HID]), ALU.subtract).then_inc(ep_centred, 1)
                gp.wait_ge(ep_rstd, s + 1)
                gp.wait_ge(ep_centred, s + 1)
                gp.tensor_tensor(adjn[:, ds(s, 1), :], ep[:, 2:3, :], eprs[:, 1:2].unsqueeze(1).broadcast_to([N, 1, HID]), ALU.mult).then_inc(ep_done, 1)

            gp.wait_ge(consts, N_CONST)
            gp.wait_ge(w2s, 5)
            degree(1)
            l0_scale(1)
            with gp.Fori(1, BATCH + 1) as s:
                gather_sq(s - 1, 1, s * GROUPS)
                weights(s - 1, 1, s * 2)
                degree(s + 1)
                l0_scale(s + 1)
                gather_sq(s, 0, s * GROUPS + HALF)
                weights(s, 0, s * 2 + 1)
                combine(s - 1)
                finish(s - 1)
            gather_sq(BATCH, 1, (BATCH + 1) * GROUPS)
            weights(BATCH, 1, (BATCH + 1) * 2)
            combine(BATCH)
            finish(BATCH)

        @block.vector
        def _(ve):
            def half_units(s, g, base):
                for e in range(UNITS // 2):
                    i = node(g, e)
                    last = ve.tensor_scalar(h[:, g % HRING, e, :], v[:, :], u[:, i:i + 1], 0.0, ALU.add, ALU.max)
                last.then_inc(h_dve, 1)

            def take_stats(g, base):
                ve.wait_ge(a_made, base + (g + 1))
                for pr in range(2):
                    last = ve.bn_stats(st[:, UNITS * g + 2 * pr:UNITS * g + 2 * pr + 2, :].rearrange("p e c -> p (e c)"),
                                       ring[:, g % PRING, pr, 0:2 * WX].rearrange("p (e w) -> p w e", e=2)[:, 0:HID, :])
                last.then_inc(a_stat, 1)

            def row_sums(s):
                ve.wait_ge(loaded, (s + 1) * 48)
                ve.reduce_sum(rsum[:, ds(s, 1)], adjn[:, ds(s, 1), :], mybir.AxisListType.X).then_inc(rsum_ready, 1)

            def scale_x(s):
                ve.wait_ge(dis_ready, s)
                ve.tensor_scalar(xs[:, :].unsqueeze(1), nodes[:, ds(s, 1), :], deg[:, 1:2], None, ALU.mult).then_inc(xs_ready, 1)

            def residual(s):
                ve.wait_ge(lin_made, s)
                ve.scalar_tensor_tensor(l0[:, 0, :], misc[:, 1, :], deg[:, 1:2], b0r[:, :], ALU.mult, ALU.add).then_inc(lin_scaled, 1)
                ve.wait_ge(lin_scaled, s)
                ve.scalar_tensor_tensor(l0[:, 1:2, :], l0[:, 0:1, :], 0.0, nodes[:, ds(s, 1), :], ALU.max, ALU.add).then_inc(res_ready, 1)
                ve.wait_ge(res_ready, s)
                ve.bn_stats(l0st[:, :], l0[:, 1, :]).then_inc(l0_stats, 1)
                wait_apart(ve, l0_stats, s)
                ve.bn_aggr(l0mv[:, :], l0st[:, :]).then_inc(l0_aggr, 1)

            def normalise(s):
                ve.wait_ge(l0_rstd, s)
                ve.tensor_scalar(x1s[:, :], l0[:, 1, :], l0mv[:, 0:1], l0rs[:, 1:2], ALU.subtract, ALU.mult).then_inc(x1_ready, 1)

            def invert(half, count):
                ve.wait_ge(sd_ready, count)
                ve.reciprocal(r0[:, half, :, :], sd[:, half, :, :]).then_inc(r0_ready, 1)

            def pick(s):
                ve.wait_ge(contracted, s * STEPS + STEPS)
                ve.wait_ge(sb2_moved, s + 1)
                for m in range(UNITS):
                    prev = sb2[:, :] if m == 0 else acc[:, m - 1, :]
                    if m:
                        ve.wait_ge(picking, s * 3 + m)
                    ve.scalar_tensor_tensor(acc[:, m, :], contr[:, m, :], diag4[:, m:m + 1], prev, ALU.mult, ALU.add)\
                      .then_inc(picking if m < UNITS - 1 else contr_free, 1)

            def end_stats(s):
                ve.wait_ge(ep_sum, s + 1)
                ve.bn_stats(epst[:, :], ep[:, 3, :]).then_inc(ep_stats, 1)
                wait_apart(ve, ep_stats, s + 1)
                ve.bn_aggr(epmv[:, :], epst[:, :]).then_inc(ep_aggr, 1)

            ve.sem_inc(a_stat, GROUPS)
            ve.sem_inc(h_dve, GROUPS)
            ve.sem_inc(r0_ready, 1)
            ve.wait_ge(consts, N_CONST)
            ve.reduce_sum(sums[:, 0:1], w2raw[:, :], mybir.AxisListType.X).then_inc(w2s, 1)
            ve.reduce_sum(sums[:, 1:2], b2raw[:, :], mybir.AxisListType.X).then_inc(b2s, 1)
            ve.wait_ge(w2s, 1)
            ve.wait_ge(b2s, 1)
            ve.tensor_scalar(sums[:, 0:2], sums[:, 0:2], -1.0 / HID, None, ALU.mult).then_inc(w2s, 1)
            ve.wait_ge(w2s, 2)
            ve.tensor_scalar(w2x[:, 0:HID], w2raw[:, :], sums[:, 0:1], None, ALU.add).then_inc(w2s, 1)
            ve.tensor_scalar(b2c[:, :], b2raw[:, :], sums[:, 1:2], None, ALU.add).then_inc(b2s, 1)
            ve.wait_ge(w2s, 3)
            ve.wait_ge(b2s, 2)
            ve.scalar_tensor_tensor(junk[:, :], w2x[:, 0:HID], 2.0, b2c[:, :], ALU.mult, ALU.mult,
                                    accum_out=w2x[:, HID:WX]).then_inc(w2s, 1)
            ve.wait_ge(w2s, 4)
            ve.scalar_tensor_tensor(junk[:, :], b2c[:, :], 1.0, b2c[:, :], ALU.mult, ALU.mult,
                                    accum_out=sums[:, 2:3]).then_inc(b2s, 1)
            ve.wait_ge(b2s, 3)
            ve.tensor_scalar(sums[:, 3:4], sums[:, 2:3], 1.0 / HID, EPS, ALU.mult, ALU.add).then_inc(w2s, 1)

            ve.wait_ge(filled, N_FILLED)
            row_sums(1)
            scale_x(1)
            residual(1)
            normalise(1)
            ve.wait_ge(uv_moved, 1)
            for g in range(LEAD):
                half_units(1, g, GROUPS)
            with ve.Fori(1, BATCH + 1) as s:
                base = ve.snap(s * GROUPS)
                for g in range(GROUPS):
                    if g + LEAD < GROUPS:
                        half_units(s, g + LEAD, base)
                    else:
                        if g + LEAD == GROUPS:
                            ve.wait_ge(uv_moved, s + 1)
                        half_units(s, g + LEAD - GROUPS, base)
                    take_stats(g, base)
                    if g == 2:
                        invert(1, s * 2)
                    if g == 3:
                        row_sums(s + 1)
                    if g == 6:
                        scale_x(s + 1)
                    if g == 13:
                        residual(s + 1)
                    if g == 16:
                        normalise(s + 1)
                    if g == 20:
                        invert(0, s * 2 + 1)
                    if g == 24:
                        pick(s - 1)
                    if g == 28:
                        end_stats(s - 1)
            invert(1, (BATCH + 1) * 2)
            pick(BATCH)
            end_stats(BATCH)

        @block.scalar
        def _(ac):
            def half_units(g):
                for e in range(UNITS // 2, UNITS):
                    i = node(g, e)
                    last = ac.activation(h[:, g % HRING, e, :], v[:, :], ACT.Relu, bias=u[:, i:i + 1])
                last.then_inc(h_act, 1)

            def move_a(g, base, s):
                if g % COLG == 0:
                    ac.wait_ge(contracted, (s - 1) * STEPS + (g // COLG + 1))
                ac.wait_ge(a_stat, base + (g + 1))
                ac.activation(a[:, g, :].rearrange("p (b w) -> p b w", b=2), ring[:, g % PRING, :, 0:2 * WX], ACT.Copy).then_inc(a_moved, 1)

            def root(half, count):
                ac.wait_ge(sq_ready, count)
                ac.activation(sd[:, half, :, :], sq[:, half, :, :], ACT.Sqrt, bias=sums[:, 3:4], scale=1.0 / HID).then_inc(sd_ready, 1)

            def move_uv(s):
                ac.wait_ge(uv_made, s)
                ac.activation(u[:, :], misc[:, 0, :], ACT.Identity, bias=b1c[:, :]).then_inc(u_moved, 1)
                ac.activation(v[:, :], misc[:, 1, :], ACT.Copy).then_inc(uv_moved, 1)
                ac.wait_ge(u_moved, s)
                ac.wait_ge(uv_moved, s)

            def move_supp(s):
                ac.wait_ge(supp_made, s)
                ac.activation(supp_t[:, :], misc[:, 0, :], ACT.Copy).then_inc(supp_moved, 1)

            def move_x1t(s):
                ac.wait_ge(x1t_made, s)
                ac.activation(x1t[:, :], misc[:, 2, :], ACT.Copy).then_inc(x1t_moved, 1)

            def move_sb2(s):
                ac.wait_ge(sb2_made, s + 1)
                ac.activation(sb2[:, :], misc[:, 3, :], ACT.Copy).then_inc(sb2_moved, 1)

            ac.sem_inc(a_moved, GROUPS)
            ac.sem_inc(h_act, GROUPS)
            ac.sem_inc(sd_ready, 1)
            ac.wait_ge(w2s, 5)
            ac.wait_ge(filled, N_FILLED)
            move_supp(1)
            move_x1t(1)
            move_uv(1)
            for g in range(LEAD):
                half_units(g)
            with ac.Fori(1, BATCH + 1) as s:
                base = ac.snap(s * GROUPS)
                for g in range(GROUPS):
                    if g + LEAD == GROUPS:
                        ac.wait_ge(h_dve, base + GROUPS)
                        ac.wait_ge(h_act, base + GROUPS)
                        move_uv(s + 1)
                    half_units((g + LEAD) % GROUPS)
                    move_a(g, base, s)
                    if g == 1:
                        root(1, s * 2)
                    if g == 6:
                        move_sb2(s - 1)
                    if g == 9:
                        move_supp(s + 1)
                    if g == 18:
                        root(0, s * 2 + 1)
                    if g == 21:
                        move_x1t(s + 1)
            root(1, (BATCH + 1) * 2)
            move_sb2(BATCH)

        @block.tensor
        def _(pe):
            def products(g, base):
                pe.wait_ge(h_dve, base + (g + 1))
                pe.wait_ge(h_act, base + (g + 1))
                if g < 2:
                    pe.wait_ge(a_moved, base - (1 - g))
                elif g >= PRING:
                    pe.wait_ge(a_moved, base + (g - PRING + 1))
                for e in range(UNITS):
                    last = pe.matmul(ring[:, g % PRING, e // 2, WX * (e % 2):WX * (e % 2 + 1)], h[:, g % HRING, e, :], w2x[:, :],
                                     start=True, stop=True)
                last.then_inc(a_made, 1)

            def contract(step, s):
                if step == 0 and not isinstance(s, int):
                    pe.wait_ge(contr_free, s)
                if step % (STEPS // 2) == 0 or step == 2:
                    pe.wait_ge(w_ready, s * 2 + (1 + step // (STEPS // 2)))
                for q in range(COLG):
                    g = COLG * step + q
                    at = ZP + ZW * g - UNITS * step
                    last = pe.matmul(contr[32 * q:32 * q + 32, :, :], z[:, at:at + ZW],
                                     a[:, g, :].rearrange("p (e w) -> p e w", w=WX)[:, :, 0:HID],
                                     start=(step == 0), stop=(step == STEPS - 1))
                last.then_inc(contracted, 1)

            def sum_b2(s):
                pe.wait_ge(w_ready, s * 2 + 2)
                pe.wait_ge(uv_moved, s + 1)
                pe.matmul(misc[:, 3, :], wn[:, :], b2c[:, :], start=True, stop=True).then_inc(sb2_made, 1)

            def support(s):
                pe.wait_ge(xs_ready, s)
                pe.wait_ge(ahat_ready, s)
                pe.matmul(misc[:, 0, :], xs[:, :], ahat_t[:, :], start=True, stop=True).then_inc(supp_made, 1)

            def linear(s):
                pe.wait_ge(supp_moved, s)
                pe.matmul(misc[:, 1, :], supp_t[:, :], w0t[:, :], start=True, stop=True).then_inc(lin_made, 1)

            def transpose_x1(s):
                pe.wait_ge(x1_ready, s)
                pe.transpose(misc[:, 2, :], x1s[:, :], ident[:, :]).then_inc(x1t_made, 1)

            def project(s):
                pe.wait_ge(x1t_moved, s)
                pe.matmul(misc[:, 0, :], w1a[:, :], x1t[:, :], start=True, stop=True)
                pe.matmul(misc[:, 1, :], w1b[:, :], x1t[:, :], start=True, stop=True).then_inc(uv_made, 1)

            pe.sem_inc(a_made, GROUPS)
            pe.wait_ge(w2s, 5)
            pe.wait_ge(filled, N_FILLED)
            support(1)
            linear(1)
            transpose_x1(1)
            project(1)
            contract(0, 0)
            contract(1, 0)
            with pe.Fori(1, BATCH + 1) as s:
                base = pe.snap(s * GROUPS)
                for g in range(GROUPS):
                    products(g, base)
                    if g % COLG == COLG - 1:
                        step, before = step_at(g)
                        contract(step, s - 1 if before else s)
                    if g == 5:
                        sum_b2(s - 1)
                    if g == 8:
                        pe.wait_ge(sb2_moved, s)
                        support(s + 1)
                    if g == 12:
                        linear(s + 1)
                    if g == 20:
                        transpose_x1(s + 1)
                    if g == 24:
                        project(s + 1)
            for step in range(2, STEPS):
                contract(step, BATCH)
                if step == STEPS // 2:
                    sum_b2(BATCH)


def kernel(x, adj, L0_gnn_W, L0_gnn_b, L1_gnn_W1, L1_gnn_b1, L1_gnn_W2, L1_gnn_b2, L1_gnn_gamma, L1_gnn_beta):
    import numpy as np
    import concourse.bacc as bacc
    from concourse.bass_utils import run_bass_kernel_spmd

    arrays = {
        "x": x, "adj": adj,
        "adj_t": np.transpose(np.asarray(adj), (0, 2, 1)),
        "w0_t": np.transpose(np.asarray(L0_gnn_W)),
        "b0": L0_gnn_b, "w1": L1_gnn_W1, "b1": L1_gnn_b1, "w2": L1_gnn_W2, "b2": L1_gnn_b2,
        "gamma": L1_gnn_gamma, "beta": L1_gnn_beta,
        "ident": np.eye(128, dtype=np.float32),
        "diag4": np.tile(np.eye(4, dtype=np.float32), (32, 1)),
    }
    arrays = {n: np.ascontiguousarray(v) for n, v in arrays.items()}
    nc = bacc.Bacc("TRN2", target_bir_lowering=False, num_devices=1)
    args = [nc.dram_tensor("in_" + n, v.shape, mybir.dt.from_np(v.dtype), kind="ExternalInput").ap() for n, v in arrays.items()]
    args.append(nc.dram_tensor("out", (64, 128, 128), mybir.dt.float32, kind="ExternalOutput").ap())
    gnn_two_layer_kernel(nc, *args)
    r = run_bass_kernel_spmd(nc, [{"in_" + n: v for n, v in arrays.items()}], core_ids=[0])
    return r.results[0]["out"]
```

```python
import concourse.bass as bass
from concourse import mybir
from contextlib import ExitStack


def gnn_two_layer_kernel(nc: bass.Bass, x, adj, adj_t, w0_t, b0, w1, b1, w2, b2, gamma, beta, ident_in, diag4_in, out):
    fp32 = mybir.dt.float32
    int32 = mybir.dt.int32
    ALU = mybir.AluOpType
    ACT = mybir.ActivationFunctionType
    ds = bass.ds

    BATCH, N, F = x.shape
    HID = w2.shape[1]
    UNITS = 4
    GROUPS = N // UNITS
    COLG = 4
    STEPS = GROUPS // COLG
    HALF = GROUPS // 2
    LEAD = 6
    HRING = 8
    EARLY = 8
    PRING = 3
    BANK = 512
    WX = HID + 1
    ZW = 32
    ZP = ZW - UNITS
    EPS = 1e-5
    NEWTON = 3
    SEED = 0x5F3759DF
    SLOTS = BATCH + 2

    ctx = ExitStack()
    with ctx:
        def sb(name, shape, dt=fp32):
            return ctx.enter_context(nc.sbuf_tensor(name, shape, dt))

        def pb(name, shape):
            return ctx.enter_context(nc.psum_tensor(name, shape, fp32))

        def sem(name):
            return ctx.enter_context(nc.semaphore(name))

        nodes = sb("nodes", [N, SLOTS, F])
        adjn = sb("adjn", [N, SLOTS, N])
        adjt = sb("adjt", [N, SLOTS, N])
        rsum = sb("rsum", [N, SLOTS])
        ident = sb("ident", [128, 128])
        diag4 = sb("diag4", [128, UNITS])
        w0t = sb("w0t", [F, F])
        w1a = sb("w1a", [F, HID])
        w1b = sb("w1b", [F, HID])
        b1c = sb("b1c", [HID, 1])
        w2raw = sb("w2raw", [HID, HID])
        w2x = sb("w2x", [HID, WX])
        b0r = sb("b0r", [N, F])
        b2raw = sb("b2raw", [N, HID])
        b2c = sb("b2c", [N, HID])
        gammar = sb("gammar", [N, HID])
        betar = sb("betar", [N, HID])
        neghalf = sb("neghalf", [N, 1])
        selfeps = sb("selfeps", [N, 1])
        junk = sb("junk", [HID, HID])
        sums = sb("sums", [HID, 4])
        deg = sb("deg", [N, 2])
        xs = sb("xs", [N, F])
        ahat_t = sb("ahat_t", [N, N])
        supp_t = sb("supp_t", [F, N])
        l0 = sb("l0", [N, 2, F])
        l0st = sb("l0st", [N, 6])
        l0mv = sb("l0mv", [N, 2])
        l0rs = sb("l0rs", [N, 2])
        x1s = sb("x1s", [N, F])
        x1t = sb("x1t", [F, N])
        uv = sb("uv", [HID, 2, 2, N])
        h = sb("h", [HID, HRING, UNITS, N])
        a = sb("a", [N, GROUPS, UNITS * WX])
        st = sb("st", [N, N, 3])
        sq = sb("sq", [N, HALF, UNITS])
        var = sb("var", [N, HALF * UNITS])
        rstd = sb("rstd", [N, NEWTON + 1, HALF * UNITS])
        nw = sb("nw", [N, 3, HALF * UNITS])
        z = sb("z", [N, ZP + ZW * GROUPS])
        wn = sb("wn", [N, N])
        sb2 = sb("sb2", [N, HID])
        acc = sb("acc", [N, UNITS, HID])
        ep = sb("ep", [N, 4, HID])
        epst = sb("epst", [N, 6])
        epmv = sb("epmv", [N, 2])
        eprs = sb("eprs", [N, 2])

        ring = pb("ring", [128, PRING, 2, BANK])
        contr = pb("contr", [128, UNITS, HID])
        misc = pb("misc", [128, 4, 128])

        h_dve = sem("h_dve")
        h_act = sem("h_act")
        a_made = sem("a_made")
        a_stat = sem("a_stat")
        a_moved = sem("a_moved")
        sq_ready = sem("sq_ready")
        var_ready = sem("var_ready")
        seeded = sem("seeded")
        newton = sem("newton")
        wn_ready = sem("wn_ready")
        w_ready = sem("w_ready")
        contracted = sem("contracted")
        loaded = sem("loaded")
        x1_kept = sem("x1_kept")
        rsum_ready = sem("rsum_ready")
        deg_ready = sem("deg_ready")
        dis_ready = sem("dis_ready")
        xs_ready = sem("xs_ready")
        ahat_ready = sem("ahat_ready")
        supp_made = sem("supp_made")
        supp_moved = sem("supp_moved")
        lin_made = sem("lin_made")
        lin_scaled = sem("lin_scaled")
        res_ready = sem("res_ready")
        l0_stats = sem("l0_stats")
        l0_aggr = sem("l0_aggr")
        l0_var = sem("l0_var")
        l0_rstd = sem("l0_rstd")
        x1_ready = sem("x1_ready")
        x1t_made = sem("x1t_made")
        x1t_moved = sem("x1t_moved")
        uv_made = sem("uv_made")
        u_moved = sem("u_moved")
        uv_moved = sem("uv_moved")
        uv_late = sem("uv_late")
        sb2_made = sem("sb2_made")
        sb2_moved = sem("sb2_moved")
        picking = sem("picking")
        contr_free = sem("contr_free")
        ep_beta = sem("ep_beta")
        ep_gamma = sem("ep_gamma")
        ep_x1 = sem("ep_x1")
        ep_sum = sem("ep_sum")
        ep_stats = sem("ep_stats")
        ep_aggr = sem("ep_aggr")
        ep_var = sem("ep_var")
        ep_rstd = sem("ep_rstd")
        ep_centred = sem("ep_centred")
        ep_done = sem("ep_done")
        consts_l0 = sem("consts_l0")
        consts = sem("consts")
        b2s = sem("b2s")
        w2s = sem("w2s")
        filled = sem("filled")
        blank_first = sem("blank_first")
        blank = sem("blank")
        stored = sem("stored")
        N_CONST = 5 * 16
        N_CONST_L0 = 6 * 16
        N_FILLED = 12
        BLANKS = (0, 2 * COLG, 16, 20, GROUPS)

        block = ctx.enter_context(nc.Block())

        def units_of_vector(g):
            return 1 if g % 16 == 3 else 2

        def node(g, e):
            return 32 * (g % COLG) + UNITS * (g // COLG) + e

        def wait_apart(eng, semaphore, value):
            value = value if isinstance(value, int) else eng.snap(eng.to_reg(value))
            eng.wait_ge(filled, N_FILLED)
            eng.wait_ge(semaphore, value)

        def step_at(g):
            k = g // COLG
            return ((k + 2), True) if k < STEPS - 2 else (k - (STEPS - 2), False)

        @block.sync
        def _(sy):
            def load(s):
                sy.dma_start(nodes[:, ds(s, 1), :], x[ds(s - 1, 1), :, :].rearrange("b n f -> n b f")).then_inc(loaded, 16)
                sy.dma_start(adjn[:, ds(s, 1), :], adj[ds(s - 1, 1), :, :].rearrange("b n f -> n b f")).then_inc(loaded, 16)
                sy.dma_start(adjt[:, ds(s, 1), :], adj_t[ds(s - 1, 1), :, :].rearrange("b n f -> n b f")).then_inc(loaded, 16)

            sy.sem_inc(loaded, 48)
            load(1)
            for dst, src in ((w2raw[:, :], w2), (b2raw[:, :], b2.unsqueeze(0).broadcast_to([N, HID])),
                             (diag4[:, :], diag4_in),
                             (gammar[:, :], gamma.unsqueeze(0).broadcast_to([N, HID])),
                             (betar[:, :], beta.unsqueeze(0).broadcast_to([N, HID]))):
                sy.dma_start(dst, src).then_inc(consts, 16)
            with sy.Fori(2, BATCH + 1) as s:
                sy.wait_ge(loaded, s * 48)
                load(s)
            sy.wait_ge(loaded, (BATCH + 1) * 48)
            sy.sem_inc(loaded, 48)
            with sy.Fori(1, BATCH + 1) as s:
                sy.wait_ge(ep_done, s + 1)
                sy.dma_start(out[ds(s - 1, 1), :, :].rearrange("b n f -> n b f"), adjn[:, ds(s, 1), :]).then_inc(stored, 16)
            sy.wait_ge(stored, 16 * BATCH)

        @block.gpsimd
        def _(gp):
            for s in (0, SLOTS - 1):
                gp.memset(nodes[:, s, :], 0.0).then_inc(filled, 1)
                gp.memset(adjn[:, s, :], 0.0).then_inc(filled, 1)
                gp.memset(adjt[:, s, :], 0.0).then_inc(filled, 1)
            gp.memset(rsum[:, 0:1], 0.0).then_inc(filled, 1)
            gp.memset(neghalf[:, :], -0.5).then_inc(filled, 1)
            gp.memset(selfeps[:, :], 1.0 + 1e-6).then_inc(filled, 1)
            gp.memset(z[:, :], 0.0).then_inc(filled, 1)
            gp.memset(wn[:, :], 0.0).then_inc(filled, 1)
            gp.memset(a[:, BLANKS[1]:BLANKS[2], :], 0.0).then_inc(blank, 1)
            gp.sem_inc(w_ready, 1)
            gp.sem_inc(sq_ready, 1)
            gp.sem_inc(x1_kept, 1)
            gp.sem_inc(wn_ready, 1)
            gp.sem_inc(newton, 4 * NEWTON)
            gp.sem_inc(var_ready, 1)
            gp.wait_ge(filled, N_FILLED)

            def degree(s):
                gp.wait_ge(rsum_ready, s)
                gp.tensor_tensor(deg[:, 0:1], rsum[:, ds(s, 1)], selfeps[:, :], ALU.add).then_inc(deg_ready, 1)
                gp.wait_ge(deg_ready, s)
                gp.tensor_tensor(deg[:, 1:2], deg[:, 0:1], neghalf[:, :], ALU.pow).then_inc(dis_ready, 1)
                gp.wait_ge(dis_ready, s)
                gp.tensor_tensor(xs[:, :].unsqueeze(1), nodes[:, ds(s, 1), :], deg[:, 1:2].unsqueeze(1).broadcast_to([N, 1, F]), ALU.mult).then_inc(xs_ready, 1)
                gp.tensor_tensor(ahat_t[:, :].unsqueeze(1), adjt[:, ds(s, 1), :], ident[:, :].unsqueeze(1), ALU.add).then_inc(ahat_ready, 1)

            def l0_scale(s):
                wait_apart(gp, l0_aggr, s)
                gp.tensor_scalar(l0rs[:, 0:1], l0mv[:, 1:2], EPS, None, ALU.add).then_inc(l0_var, 1)
                gp.wait_ge(l0_var, s)
                gp.tensor_tensor(l0rs[:, 1:2], l0rs[:, 0:1], neghalf[:, :], ALU.pow).then_inc(l0_rstd, 1)

            def keep_x1(s):
                wait_apart(gp, x1_ready, s)
                gp.tensor_copy(nodes[:, ds(s, 1), :], x1s[:, :].unsqueeze(1)).then_inc(x1_kept, 1)

            def copy_uv(s, read):
                if read is not None:
                    read = gp.snap(gp.to_reg(read))
                wait_apart(gp, uv_moved, s)
                if read is not None:
                    gp.wait_ge(h_dve, read)
                    gp.wait_ge(h_act, read)
                gp.tensor_copy(uv[:, 1, :, :], uv[:, 0, :, :]).then_inc(uv_late, 1)

            def gather_var(s, half, count, taken):
                gp.wait_ge(a_stat, taken)
                n0 = half * HALF * UNITS
                gp.tensor_tensor(sq[:, :, :], st[:, n0:n0 + HALF * UNITS, 2].rearrange("p (g e) -> p g e", e=UNITS),
                                 a[:, half * HALF:(half + 1) * HALF, :].rearrange("p g (e w) -> p g e w", w=WX)[:, :, :, HID],
                                 ALU.add).then_inc(sq_ready, 1)
                wait_apart(gp, sq_ready, count)
                gp.tensor_scalar(var[:, :], sq[:, :, :].rearrange("p g e -> p (g e)"), 1.0 / HID, sums[:, 3:4], ALU.mult, ALU.add).then_inc(var_ready, 1)

            def weights(s, half, count):
                gp.wait_ge(seeded, count)
                k = (count - 1) * (4 * NEWTON)
                for n in range(NEWTON):
                    if n:
                        gp.wait_ge(newton, k + 4 * n)
                    r = rstd[:, n, :]
                    gp.tensor_tensor(nw[:, 0, :], r, r, ALU.mult).then_inc(newton, 1)
                    gp.wait_ge(newton, k + (4 * n + 1))
                    gp.tensor_tensor(nw[:, 1, :], nw[:, 0, :], var[:, :], ALU.mult).then_inc(newton, 1)
                    wait_apart(gp, newton, k + (4 * n + 2))
                    gp.tensor_scalar(nw[:, 2, :], nw[:, 1, :], -0.5, 1.5, ALU.mult, ALU.add).then_inc(newton, 1)
                    gp.wait_ge(newton, k + (4 * n + 3))
                    gp.tensor_tensor(rstd[:, n + 1, :], nw[:, 2, :], r, ALU.mult).then_inc(newton, 1)
                gp.wait_ge(newton, k + 4 * NEWTON)
                if half == 0:
                    gp.wait_ge(sb2_made, s)
                C = HALF // COLG
                at = half * C * UNITS
                adj_v = adjt[:, ds(s, 1), :].rearrange("p o (q r) -> p (o q) r", q=COLG)[:, :, at:at + C * UNITS]
                w_v = wn[:, :].rearrange("p (q r) -> p q r", q=COLG)[:, :, at:at + C * UNITS]
                gp.tensor_tensor(w_v.rearrange("p q (c e) -> p q c e", e=UNITS), adj_v.rearrange("p q (c e) -> p q c e", e=UNITS),
                                 rstd[:, NEWTON, :].rearrange("p (c q e) -> p q c e", q=COLG, e=UNITS), ALU.mult).then_inc(wn_ready, 1)
                wait_apart(gp, wn_ready, count)
                z_v = z[:, ZW * half * HALF:ZW * (half + 1) * HALF].rearrange("p (c q r) -> p c q r", q=COLG, r=ZW)[:, :, :, ZP:ZW]
                gp.tensor_copy(z_v, w_v.rearrange("p q (c e) -> p c q e", e=UNITS)).then_inc(w_ready, 1)

            def combine(s):
                gp.tensor_tensor(ep[:, 0, :], betar[:, :], rsum[:, ds(s, 1)].broadcast_to([N, HID]), ALU.mult).then_inc(ep_beta, 1)
                gp.wait_ge(contr_free, s + 1)
                gp.tensor_tensor(ep[:, 1, :], acc[:, UNITS - 1, :], gammar[:, :], ALU.mult).then_inc(ep_gamma, 1)
                gp.wait_ge(ep_gamma, s + 1)
                gp.wait_ge(ep_beta, s + 1)
                gp.wait_ge(x1_kept, s + 1)
                gp.tensor_tensor(ep[:, 2:3, :], ep[:, 1:2, :], nodes[:, ds(s, 1), :], ALU.add).then_inc(ep_x1, 1)
                gp.wait_ge(ep_x1, s + 1)
                gp.tensor_tensor(ep[:, 3, :], ep[:, 2, :], ep[:, 0, :], ALU.add).then_inc(ep_sum, 1)

            def finish(s):
                wait_apart(gp, ep_aggr, s + 1)
                gp.tensor_scalar(eprs[:, 0:1], epmv[:, 1:2], EPS, None, ALU.add).then_inc(ep_var, 1)
                gp.wait_ge(ep_var, s + 1)
                gp.tensor_tensor(eprs[:, 1:2], eprs[:, 0:1], neghalf[:, :], ALU.pow).then_inc(ep_rstd, 1)
                gp.tensor_tensor(ep[:, 2, :], ep[:, 3, :], epmv[:, 0:1].broadcast_to([N, HID]), ALU.subtract).then_inc(ep_centred, 1)
                gp.wait_ge(ep_rstd, s + 1)
                gp.wait_ge(ep_centred, s + 1)
                gp.tensor_tensor(adjn[:, ds(s, 1), :], ep[:, 2:3, :], eprs[:, 1:2].unsqueeze(1).broadcast_to([N, 1, HID]), ALU.mult).then_inc(ep_done, 1)

            gp.wait_ge(consts_l0, N_CONST_L0)
            degree(1)
            gp.memset(a[:, BLANKS[3]:BLANKS[4], :], 0.0).then_inc(blank, 1)
            l0_scale(1)
            keep_x1(1)
            copy_uv(1, None)
            gp.wait_ge(w2s, 5)
            with gp.Fori(1, BATCH + 1) as s:
                gather_var(s - 1, 1, s * 2, s * GROUPS)
                degree(s + 1)
                weights(s - 1, 1, s * 2)
                l0_scale(s + 1)
                gather_var(s, 0, s * 2 + 1, s * GROUPS + HALF)
                keep_x1(s + 1)
                weights(s, 0, s * 2 + 1)
                combine(s - 1)
                finish(s - 1)
                copy_uv(s + 1, (s + 1) * GROUPS)
            gather_var(BATCH, 1, (BATCH + 1) * 2, (BATCH + 1) * GROUPS)
            weights(BATCH, 1, (BATCH + 1) * 2)
            combine(BATCH)
            finish(BATCH)

        @block.vector
        def _(ve):
            def half_units(g):
                late = int(g >= EARLY)
                for e in range(units_of_vector(g)):
                    i = node(g, e)
                    last = ve.tensor_scalar(h[:, g % HRING, e, :], uv[:, late, 1, :], uv[:, late, 0, i:i + 1], 0.0, ALU.add, ALU.max)
                last.then_inc(h_dve, 1)

            def take_stats(g, count):
                ve.wait_ge(a_moved, count)
                for pr in range(2):
                    last = ve.bn_stats(st[:, UNITS * g + 2 * pr:UNITS * g + 2 * pr + 2, :].rearrange("p e c -> p (e c)"),
                                       a[:, g, 2 * pr * WX:2 * (pr + 1) * WX].rearrange("p (e w) -> p w e", e=2)[:, 0:HID, :])
                last.then_inc(a_stat, 1)

            def row_sums(s):
                ve.wait_ge(loaded, (s + 1) * 48)
                ve.reduce_sum(rsum[:, ds(s, 1)], adjn[:, ds(s, 1), :], mybir.AxisListType.X).then_inc(rsum_ready, 1)

            def residual(s, part):
                if part == 0:
                    ve.wait_ge(lin_made, s)
                    ve.scalar_tensor_tensor(l0[:, 0, :], misc[:, 1, :], deg[:, 1:2], b0r[:, :], ALU.mult, ALU.add).then_inc(lin_scaled, 1)
                elif part == 1:
                    ve.wait_ge(lin_scaled, s)
                    ve.scalar_tensor_tensor(l0[:, 1:2, :], l0[:, 0:1, :], 0.0, nodes[:, ds(s, 1), :], ALU.max, ALU.add).then_inc(res_ready, 1)
                elif part == 2:
                    ve.wait_ge(res_ready, s)
                    ve.bn_stats(l0st[:, :], l0[:, 1, :]).then_inc(l0_stats, 1)
                else:
                    wait_apart(ve, l0_stats, s)
                    ve.bn_aggr(l0mv[:, :], l0st[:, :]).then_inc(l0_aggr, 1)

            def normalise(s):
                ve.wait_ge(l0_rstd, s)
                ve.tensor_scalar(x1s[:, :], l0[:, 1, :], l0mv[:, 0:1], l0rs[:, 1:2], ALU.subtract, ALU.mult).then_inc(x1_ready, 1)

            def seed(count):
                ve.wait_ge(var_ready, count)
                ve.tensor_scalar(rstd[:, 0, :].bitcast(int32), var[:, :].bitcast(int32), -0.5, float(SEED), ALU.mult, ALU.add).then_inc(seeded, 1)

            def pick(s, m):
                if m == 0:
                    ve.wait_ge(contracted, s * STEPS + STEPS)
                    ve.wait_ge(sb2_moved, s + 1)
                else:
                    ve.wait_ge(picking, s * 3 + m)
                prev = sb2[:, :] if m == 0 else acc[:, m - 1, :]
                ve.scalar_tensor_tensor(acc[:, m, :], contr[:, m, :], diag4[:, m:m + 1], prev, ALU.mult, ALU.add)\
                  .then_inc(picking if m < UNITS - 1 else contr_free, 1)

            def end_stats(s, part):
                if part == 0:
                    ve.wait_ge(ep_sum, s + 1)
                    ve.bn_stats(epst[:, :], ep[:, 3, :]).then_inc(ep_stats, 1)
                else:
                    wait_apart(ve, ep_stats, s + 1)
                    ve.bn_aggr(epmv[:, :], epst[:, :]).then_inc(ep_aggr, 1)

            ve.memset(st[:, :, :], 0.0).then_inc(filled, 1)
            ve.memset(a[:, BLANKS[0]:BLANKS[1], :], 0.0).then_inc(blank_first, 1)
            ve.sem_inc(a_stat, GROUPS - 1)
            ve.sem_inc(h_dve, GROUPS)
            ve.sem_inc(seeded, 1)
            ve.wait_ge(filled, N_FILLED)
            row_sums(1)
            ve.wait_ge(consts, N_CONST)
            ve.reduce_sum(sums[:, 0:1], w2raw[:, :], mybir.AxisListType.X).then_inc(w2s, 1)
            ve.reduce_sum(sums[:, 1:2], b2raw[:, :], mybir.AxisListType.X).then_inc(b2s, 1)
            ve.wait_ge(w2s, 1)
            ve.wait_ge(b2s, 1)
            ve.tensor_scalar(sums[:, 0:2], sums[:, 0:2], -1.0 / HID, None, ALU.mult).then_inc(w2s, 1)
            ve.wait_ge(w2s, 2)
            ve.tensor_scalar(w2x[:, 0:HID], w2raw[:, :], sums[:, 0:1], None, ALU.add).then_inc(w2s, 1)
            ve.tensor_scalar(b2c[:, :], b2raw[:, :], sums[:, 1:2], None, ALU.add).then_inc(b2s, 1)
            ve.wait_ge(w2s, 3)
            ve.wait_ge(b2s, 2)
            ve.scalar_tensor_tensor(junk[:, :], w2x[:, 0:HID], 2.0, b2c[:, :], ALU.mult, ALU.mult,
                                    accum_out=w2x[:, HID:WX]).then_inc(w2s, 1)
            ve.wait_ge(w2s, 4)
            ve.scalar_tensor_tensor(junk[:, :], b2c[:, :], 1.0, b2c[:, :], ALU.mult, ALU.mult,
                                    accum_out=sums[:, 2:3]).then_inc(b2s, 1)
            ve.wait_ge(b2s, 3)
            ve.tensor_scalar(sums[:, 3:4], sums[:, 2:3], 1.0 / HID, EPS, ALU.mult, ALU.add).then_inc(w2s, 1)

            ve.memset(a[:, BLANKS[2]:BLANKS[3], :], 0.0).then_inc(blank, 1)
            ve.wait_ge(consts_l0, N_CONST_L0)
            for part in range(4):
                residual(1, part)
            normalise(1)
            ve.wait_ge(uv_moved, 1)
            for g in range(LEAD):
                half_units(g)
            with ve.Fori(1, BATCH + 1) as s:
                base = ve.snap(s * GROUPS)
                for g in range(GROUPS):
                    ahead = (g + LEAD) % GROUPS
                    if g + LEAD == GROUPS:
                        ve.wait_ge(uv_moved, s + 1)
                    if ahead == EARLY:
                        ve.wait_ge(uv_late, s)
                    if g == 0:
                        row_sums(s + 1)
                    if g == 4:
                        seed(s * 2)
                    if 13 <= g < 17:
                        residual(s + 1, g - 13)
                    if g == 18:
                        normalise(s + 1)
                    if g == 20:
                        seed(s * 2 + 1)
                    if g in (24, 25):
                        pick(s - 1, 2 * (g - 24))
                    if g in (29, 31):
                        end_stats(s - 1, (g - 29) // 2)
                    half_units(ahead)
                    if g in (24, 25):
                        pick(s - 1, 2 * (g - 24) + 1)
                    take_stats((g - 1) % GROUPS, base + g)
            take_stats(GROUPS - 1, (BATCH + 1) * GROUPS)
            seed((BATCH + 1) * 2)
            for m in range(UNITS):
                pick(BATCH, m)
            for part in range(2):
                end_stats(BATCH, part)

        @block.scalar
        def _(ac):
            def half_units(g):
                late = int(g >= EARLY)
                for e in range(units_of_vector(g), UNITS):
                    i = node(g, e)
                    last = ac.activation(h[:, g % HRING, e, :], uv[:, late, 1, :], ACT.Relu, bias=uv[:, late, 0, i:i + 1])
                last.then_inc(h_act, 1)

            def move_a(g, base, s):
                if g % COLG == 0:
                    ac.wait_ge(contracted, (s - 1) * STEPS + (g // COLG + 1))
                ac.wait_ge(a_made, base + (g + 1))
                ac.activation(a[:, g, :].rearrange("p (b w) -> p b w", b=2), ring[:, g % PRING, :, 0:2 * WX], ACT.Copy).then_inc(a_moved, 1)

            def move_uv(s):
                ac.wait_ge(uv_made, s)
                ac.activation(uv[:, 0, 0, :], misc[:, 0, :], ACT.Identity, bias=b1c[:, :]).then_inc(u_moved, 1)
                ac.activation(uv[:, 0, 1, :], misc[:, 1, :], ACT.Copy).then_inc(uv_moved, 1)
                ac.wait_ge(u_moved, s)
                ac.wait_ge(uv_moved, s)

            def move_supp(s):
                ac.wait_ge(supp_made, s)
                ac.activation(supp_t[:, :], misc[:, 0, :], ACT.Copy).then_inc(supp_moved, 1)

            def move_x1t(s):
                ac.wait_ge(x1t_made, s)
                ac.activation(x1t[:, :], misc[:, 2, :], ACT.Copy).then_inc(x1t_moved, 1)

            def move_sb2(s):
                ac.wait_ge(sb2_made, s + 1)
                ac.activation(sb2[:, :], misc[:, 3, :], ACT.Copy).then_inc(sb2_moved, 1)

            for dst, src in ((ident[:, :], ident_in), (w0t[:, :], w0_t),
                             (b0r[:, :], b0.unsqueeze(0).broadcast_to([N, F])),
                             (w1a[:, :], w1[0:F, :]), (w1b[:, :], w1[F:2 * F, :]), (b1c[:, :], b1.unsqueeze(1))):
                ac.dma_start(dst, src).then_inc(consts_l0, 16)
            ac.sem_inc(a_moved, GROUPS)
            ac.sem_inc(h_act, GROUPS)
            ac.wait_ge(consts_l0, N_CONST_L0)
            ac.wait_ge(filled, N_FILLED)
            move_supp(1)
            ac.wait_ge(blank_first, 1)
            ac.wait_ge(blank, 3)
            move_x1t(1)
            move_uv(1)
            for g in range(LEAD):
                half_units(g)
            with ac.Fori(1, BATCH + 1) as s:
                base = ac.snap(s * GROUPS)
                for g in range(GROUPS):
                    ahead = (g + LEAD) % GROUPS
                    if ahead == EARLY:
                        ac.wait_ge(uv_late, s)
                    half_units(ahead)
                    if g == 10:
                        move_supp(s + 1)
                    if g == 16:
                        move_sb2(s - 1)
                    if g == 21:
                        move_x1t(s + 1)
                    if g == 24:
                        ac.wait_ge(h_dve, base + EARLY)
                        ac.wait_ge(h_act, base + EARLY)
                        ac.wait_ge(uv_late, s)
                        move_uv(s + 1)
                    move_a(g, base, s)
            move_sb2(BATCH)

        @block.tensor
        def _(pe):
            def products(g, base):
                pe.wait_ge(h_dve, base + (g + 1))
                pe.wait_ge(h_act, base + (g + 1))
                if g < 2:
                    pe.wait_ge(a_moved, base - (1 - g))
                elif g >= PRING:
                    pe.wait_ge(a_moved, base + (g - PRING + 1))
                for e in range(UNITS):
                    last = pe.matmul(ring[:, g % PRING, e // 2, WX * (e % 2):WX * (e % 2 + 1)], h[:, g % HRING, e, :], w2x[:, :],
                                     start=True, stop=True)
                last.then_inc(a_made, 1)

            def contract(step, s):
                if step == 0 and not isinstance(s, int):
                    pe.wait_ge(contr_free, s)
                if step % (STEPS // 2) == 0 or step == 2:
                    pe.wait_ge(w_ready, s * 2 + (1 + step // (STEPS // 2)))
                for q in range(COLG):
                    g = COLG * step + q
                    at = ZP + ZW * g - UNITS * step
                    last = pe.matmul(contr[32 * q:32 * q + 32, :, :], z[:, at:at + ZW],
                                     a[:, g, :].rearrange("p (e w) -> p e w", w=WX)[:, :, 0:HID],
                                     start=(step == 0), stop=(step == STEPS - 1))
                last.then_inc(contracted, 1)

            def sum_b2(s):
                pe.wait_ge(w_ready, s * 2 + 2)
                pe.matmul(misc[:, 3, :], wn[:, :], b2c[:, :], start=True, stop=True).then_inc(sb2_made, 1)

            def support(s):
                pe.wait_ge(xs_ready, s)
                pe.wait_ge(ahat_ready, s)
                if not isinstance(s, int):
                    pe.wait_ge(uv_moved, s - 1)
                pe.matmul(misc[:, 0, :], xs[:, :], ahat_t[:, :], start=True, stop=True).then_inc(supp_made, 1)

            def linear(s):
                pe.wait_ge(supp_moved, s)
                pe.matmul(misc[:, 1, :], supp_t[:, :], w0t[:, :], start=True, stop=True).then_inc(lin_made, 1)

            def transpose_x1(s):
                pe.wait_ge(x1_ready, s)
                pe.transpose(misc[:, 2, :], x1s[:, :], ident[:, :]).then_inc(x1t_made, 1)

            def project(s):
                pe.wait_ge(x1t_moved, s)
                pe.matmul(misc[:, 0, :], w1a[:, :], x1t[:, :], start=True, stop=True)
                pe.matmul(misc[:, 1, :], w1b[:, :], x1t[:, :], start=True, stop=True).then_inc(uv_made, 1)

            pe.sem_inc(a_made, GROUPS)
            pe.wait_ge(filled, N_FILLED)
            pe.wait_ge(blank_first, 1)
            contract(0, 0)
            contract(1, 0)
            pe.wait_ge(consts_l0, N_CONST_L0)
            support(1)
            linear(1)
            transpose_x1(1)
            project(1)
            pe.wait_ge(blank, 3)
            pe.wait_ge(w2s, 5)
            with pe.Fori(1, BATCH + 1) as s:
                base = pe.snap(s * GROUPS)
                for g in range(GROUPS):
                    products(g, base)
                    if g % COLG == COLG - 1:
                        step, before = step_at(g)
                        contract(step, s - 1 if before else s)
                    if g == 9:
                        support(s + 1)
                    if g == 12:
                        linear(s + 1)
                    if g == 15:
                        pe.wait_ge(lin_scaled, s + 1)
                        sum_b2(s - 1)
                    if g == 20:
                        pe.wait_ge(sb2_moved, s)
                        transpose_x1(s + 1)
                    if g == 22:
                        project(s + 1)
            for step in range(2, STEPS):
                contract(step, BATCH)
                if step == STEPS // 2:
                    pe.wait_ge(uv_moved, BATCH + 1)
                    sum_b2(BATCH)


def kernel(x, adj, L0_gnn_W, L0_gnn_b, L1_gnn_W1, L1_gnn_b1, L1_gnn_W2, L1_gnn_b2, L1_gnn_gamma, L1_gnn_beta):
    import numpy as np
    import concourse.bacc as bacc
    from concourse.bass_utils import run_bass_kernel_spmd

    arrays = {
        "x": x, "adj": adj,
        "adj_t": np.transpose(np.asarray(adj), (0, 2, 1)),
        "w0_t": np.transpose(np.asarray(L0_gnn_W)),
        "b0": L0_gnn_b, "w1": L1_gnn_W1, "b1": L1_gnn_b1, "w2": L1_gnn_W2, "b2": L1_gnn_b2,
        "gamma": L1_gnn_gamma, "beta": L1_gnn_beta,
        "ident": np.eye(128, dtype=np.float32),
        "diag4": np.tile(np.eye(4, dtype=np.float32), (32, 1)),
    }
    arrays = {n: np.ascontiguousarray(v) for n, v in arrays.items()}
    nc = bacc.Bacc("TRN2", target_bir_lowering=False, num_devices=1)
    args = [nc.dram_tensor("in_" + n, v.shape, mybir.dt.from_np(v.dtype), kind="ExternalInput").ap() for n, v in arrays.items()]
    args.append(nc.dram_tensor("out", (64, 128, 128), mybir.dt.float32, kind="ExternalOutput").ap())
    gnn_two_layer_kernel(nc, *args)
    r = run_bass_kernel_spmd(nc, [{"in_" + n: v for n, v in arrays.items()}], core_ids=[0])
    return r.results[0]["out"]
```

```python
import concourse.bass as bass
from concourse import mybir
from contextlib import ExitStack


def gnn_two_layer_kernel(nc: bass.Bass, x, adj, adj_t, w0_t, b0, w1, b1, w2, b2, gamma, beta, ident_in, diag4_in, out):
    fp32 = mybir.dt.float32
    int32 = mybir.dt.int32
    ALU = mybir.AluOpType
    ACT = mybir.ActivationFunctionType
    ds = bass.ds

    BATCH, N, F = x.shape
    HID = w2.shape[1]
    UNITS = 4
    VUNITS = 2
    GROUPS = N // UNITS
    COLG = 4
    STEPS = GROUPS // COLG
    HALF = GROUPS // 2
    LEAD = 6
    HRING = 8
    EARLY = 8
    PRING = 3
    BANK = 512
    WX = HID + 1
    ZW = 32
    ZP = ZW - UNITS
    EPS = 1e-5
    NEWTON = 3
    SEED = 0x5F3759DF
    SLOTS = BATCH + 2

    ctx = ExitStack()
    with ctx:
        def sb(name, shape, dt=fp32):
            return ctx.enter_context(nc.sbuf_tensor(name, shape, dt))

        def pb(name, shape):
            return ctx.enter_context(nc.psum_tensor(name, shape, fp32))

        def sem(name):
            return ctx.enter_context(nc.semaphore(name))

        nodes = sb("nodes", [N, SLOTS, F])
        adjn = sb("adjn", [N, SLOTS, N])
        adjt = sb("adjt", [N, SLOTS, N])
        rsum = sb("rsum", [N, SLOTS])
        ident = sb("ident", [128, 128])
        diag4 = sb("diag4", [128, UNITS])
        w0t = sb("w0t", [F, F])
        w1a = sb("w1a", [F, HID])
        w1b = sb("w1b", [F, HID])
        b1c = sb("b1c", [HID, 1])
        w2raw = sb("w2raw", [HID, HID])
        w2x = sb("w2x", [HID, WX])
        b0r = sb("b0r", [N, F])
        b2raw = sb("b2raw", [N, HID])
        b2c = sb("b2c", [N, HID])
        gammar = sb("gammar", [N, HID])
        betar = sb("betar", [N, HID])
        neghalf = sb("neghalf", [N, 1])
        ones = sb("ones", [N, 1])
        selfeps = sb("selfeps", [N, 1])
        junk = sb("junk", [HID, HID])
        sums = sb("sums", [HID, 4])
        deg = sb("deg", [N, 2])
        xs = sb("xs", [N, F])
        ahat_t = sb("ahat_t", [N, N])
        supp_t = sb("supp_t", [F, N])
        l0 = sb("l0", [N, 2, F])
        l0st = sb("l0st", [N, 6])
        l0mv = sb("l0mv", [N, 2])
        l0rs = sb("l0rs", [N, 2])
        x1s = sb("x1s", [N, F])
        x1t = sb("x1t", [F, N])
        uv = sb("uv", [HID, 2, 2, N])
        h = sb("h", [HID, HRING, UNITS, N])
        a = sb("a", [N, GROUPS, UNITS * WX])
        st = sb("st", [N, N, 3])
        sq = sb("sq", [N, HALF, UNITS])
        var_raw = sb("var_raw", [N, HALF * UNITS])
        var = sb("var", [N, HALF * UNITS])
        rstd = sb("rstd", [N, NEWTON + 1, HALF * UNITS])
        nw = sb("nw", [N, 3, HALF * UNITS])
        z = sb("z", [N, ZP + ZW * GROUPS])
        wn = sb("wn", [N, N])
        wsum = sb("wsum", [N, 1])
        sb2 = sb("sb2", [N, HID])
        acc = sb("acc", [N, UNITS, HID])
        ep = sb("ep", [N, 4, HID])
        epst = sb("epst", [N, 6])
        epmv = sb("epmv", [N, 2])
        eprs = sb("eprs", [N, 2])

        ring = pb("ring", [128, PRING, 2, BANK])
        contr = pb("contr", [128, UNITS, HID])
        misc = pb("misc", [128, 4, 128])

        h_dve = sem("h_dve")
        h_act = sem("h_act")
        a_made = sem("a_made")
        a_stat = sem("a_stat")
        a_moved = sem("a_moved")
        sq_ready = sem("sq_ready")
        raw_ready = sem("raw_ready")
        var_ready = sem("var_ready")
        seeded = sem("seeded")
        newton = sem("newton")
        wn_ready = sem("wn_ready")
        w_ready = sem("w_ready")
        contracted = sem("contracted")
        loaded = sem("loaded")
        x1_kept = sem("x1_kept")
        rsum_ready = sem("rsum_ready")
        deg_ready = sem("deg_ready")
        dis_ready = sem("dis_ready")
        xs_ready = sem("xs_ready")
        ahat_ready = sem("ahat_ready")
        supp_made = sem("supp_made")
        supp_moved = sem("supp_moved")
        lin_made = sem("lin_made")
        lin_scaled = sem("lin_scaled")
        res_ready = sem("res_ready")
        l0_stats = sem("l0_stats")
        l0_aggr = sem("l0_aggr")
        l0_var = sem("l0_var")
        l0_rstd = sem("l0_rstd")
        l0_centred = sem("l0_centred")
        x1_ready = sem("x1_ready")
        x1t_made = sem("x1t_made")
        x1t_moved = sem("x1t_moved")
        uv_made = sem("uv_made")
        u_moved = sem("u_moved")
        uv_moved = sem("uv_moved")
        uv_late = sem("uv_late")
        wsum_made = sem("wsum_made")
        wsum_moved = sem("wsum_moved")
        sb2_ready = sem("sb2_ready")
        picking = sem("picking")
        contr_free = sem("contr_free")
        ep_beta = sem("ep_beta")
        ep_gamma = sem("ep_gamma")
        ep_x1 = sem("ep_x1")
        ep_sum = sem("ep_sum")
        ep_stats = sem("ep_stats")
        ep_aggr = sem("ep_aggr")
        ep_var = sem("ep_var")
        ep_rstd = sem("ep_rstd")
        ep_centred = sem("ep_centred")
        ep_done = sem("ep_done")
        consts_l0 = sem("consts_l0")
        consts = sem("consts")
        b2s = sem("b2s")
        w2s = sem("w2s")
        filled = sem("filled")
        blank_first = sem("blank_first")
        blank = sem("blank")
        stored = sem("stored")
        N_CONST = 5 * 16
        N_CONST_L0 = 6 * 16
        N_FILLED = 13
        BLANKS = (0, 2 * COLG, 16, 20, GROUPS)

        block = ctx.enter_context(nc.Block())

        def node(g, e):
            return 32 * (g % COLG) + UNITS * (g // COLG) + e

        def wait_apart(eng, semaphore, value):
            value = value if isinstance(value, int) else eng.snap(eng.to_reg(value))
            eng.wait_ge(filled, N_FILLED)
            eng.wait_ge(semaphore, value)

        def step_at(g):
            k = g // COLG
            return ((k + 2), True) if k < STEPS - 2 else (k - (STEPS - 2), False)

        @block.sync
        def _(sy):
            def load(s):
                sy.dma_start(nodes[:, ds(s, 1), :], x[ds(s - 1, 1), :, :].rearrange("b n f -> n b f")).then_inc(loaded, 16)
                sy.dma_start(adjn[:, ds(s, 1), :], adj[ds(s - 1, 1), :, :].rearrange("b n f -> n b f")).then_inc(loaded, 16)
                sy.dma_start(adjt[:, ds(s, 1), :], adj_t[ds(s - 1, 1), :, :].rearrange("b n f -> n b f")).then_inc(loaded, 16)

            sy.sem_inc(loaded, 48)
            load(1)
            for dst, src in ((w2raw[:, :], w2), (b2raw[:, :], b2.unsqueeze(0).broadcast_to([N, HID])),
                             (diag4[:, :], diag4_in),
                             (gammar[:, :], gamma.unsqueeze(0).broadcast_to([N, HID])),
                             (betar[:, :], beta.unsqueeze(0).broadcast_to([N, HID]))):
                sy.dma_start(dst, src).then_inc(consts, 16)
            with sy.Fori(2, BATCH + 1) as s:
                sy.wait_ge(loaded, s * 48)
                load(s)
            sy.wait_ge(loaded, (BATCH + 1) * 48)
            sy.sem_inc(loaded, 48)
            with sy.Fori(1, BATCH + 1) as s:
                sy.wait_ge(ep_done, s + 1)
                sy.dma_start(out[ds(s - 1, 1), :, :].rearrange("b n f -> n b f"), adjn[:, ds(s, 1), :]).then_inc(stored, 16)
            sy.wait_ge(stored, 16 * BATCH)

        @block.gpsimd
        def _(gp):
            for s in (0, SLOTS - 1):
                gp.memset(nodes[:, s, :], 0.0).then_inc(filled, 1)
                gp.memset(adjn[:, s, :], 0.0).then_inc(filled, 1)
                gp.memset(adjt[:, s, :], 0.0).then_inc(filled, 1)
            gp.memset(rsum[:, 0:1], 0.0).then_inc(filled, 1)
            gp.memset(neghalf[:, :], -0.5).then_inc(filled, 1)
            gp.memset(ones[:, :], 1.0).then_inc(filled, 1)
            gp.memset(selfeps[:, :], 1.0 + 1e-6).then_inc(filled, 1)
            gp.memset(z[:, :], 0.0).then_inc(filled, 1)
            gp.memset(wn[:, :], 0.0).then_inc(filled, 1)
            gp.memset(a[:, BLANKS[1]:BLANKS[2], :], 0.0).then_inc(blank, 1)
            gp.sem_inc(w_ready, 1)
            gp.sem_inc(sq_ready, 1)
            gp.sem_inc(raw_ready, 1)
            gp.sem_inc(x1_kept, 1)
            gp.sem_inc(wn_ready, 1)
            gp.sem_inc(newton, 4 * NEWTON)
            gp.sem_inc(var_ready, 1)
            gp.wait_ge(filled, N_FILLED)

            def degree(s):
                gp.wait_ge(rsum_ready, s)
                gp.tensor_tensor(deg[:, 0:1], rsum[:, ds(s, 1)], selfeps[:, :], ALU.add).then_inc(deg_ready, 1)
                gp.wait_ge(deg_ready, s)
                gp.tensor_tensor(deg[:, 1:2], deg[:, 0:1], neghalf[:, :], ALU.pow).then_inc(dis_ready, 1)
                gp.wait_ge(dis_ready, s)
                gp.tensor_tensor(xs[:, :].unsqueeze(1), nodes[:, ds(s, 1), :], deg[:, 1:2].unsqueeze(1).broadcast_to([N, 1, F]), ALU.mult).then_inc(xs_ready, 1)
                gp.tensor_tensor(ahat_t[:, :].unsqueeze(1), adjt[:, ds(s, 1), :], ident[:, :].unsqueeze(1), ALU.add).then_inc(ahat_ready, 1)

            def normalise(s):
                wait_apart(gp, l0_aggr, s)
                gp.tensor_scalar(l0rs[:, 0:1], l0mv[:, 1:2], EPS, None, ALU.add).then_inc(l0_var, 1)
                gp.wait_ge(l0_var, s)
                gp.tensor_tensor(l0rs[:, 1:2], l0rs[:, 0:1], neghalf[:, :], ALU.pow).then_inc(l0_rstd, 1)
                gp.tensor_tensor(l0[:, 0, :], l0[:, 1, :], l0mv[:, 0:1].broadcast_to([N, F]), ALU.subtract).then_inc(l0_centred, 1)
                gp.wait_ge(l0_rstd, s)
                gp.wait_ge(l0_centred, s)
                if not isinstance(s, int):
                    gp.wait_ge(x1t_made, s - 1)
                gp.tensor_tensor(x1s[:, :], l0[:, 0, :], l0rs[:, 1:2].broadcast_to([N, F]), ALU.mult).then_inc(x1_ready, 1)

            def keep_x1(s):
                wait_apart(gp, x1_ready, s)
                gp.tensor_copy(nodes[:, ds(s, 1), :], x1s[:, :].unsqueeze(1)).then_inc(x1_kept, 1)

            def gather_var(s, half, count, taken):
                gp.wait_ge(a_stat, taken)
                n0 = half * HALF * UNITS
                gp.tensor_tensor(sq[:, :, :].rearrange("p g (b e) -> p (g b) e", e=2), st[:, n0:n0 + HALF * UNITS, 2].rearrange("p (g e) -> p g e", e=2),
                                 a[:, half * HALF:(half + 1) * HALF, :].rearrange("p g (b w e) -> p (g b) w e", b=2, e=2)[:, :, HID, :],
                                 ALU.add).then_inc(sq_ready, 1)
                wait_apart(gp, sq_ready, count)
                gp.tensor_scalar(var_raw[:, :], sq[:, :, :].rearrange("p g e -> p (g e)"), 1.0 / HID, sums[:, 3:4], ALU.mult, ALU.add).then_inc(raw_ready, 1)
                wait_apart(gp, raw_ready, count)
                gp.tensor_scalar(var[:, :], var_raw[:, :], EPS, None, ALU.max).then_inc(var_ready, 1)

            def weights(s, half, count):
                gp.wait_ge(seeded, count)
                k = (count - 1) * (4 * NEWTON)
                for n in range(NEWTON):
                    if n:
                        gp.wait_ge(newton, k + 4 * n)
                    r = rstd[:, n, :]
                    gp.tensor_tensor(nw[:, 0, :], r, r, ALU.mult).then_inc(newton, 1)
                    gp.wait_ge(newton, k + (4 * n + 1))
                    gp.tensor_tensor(nw[:, 1, :], nw[:, 0, :], var[:, :], ALU.mult).then_inc(newton, 1)
                    wait_apart(gp, newton, k + (4 * n + 2))
                    gp.tensor_scalar(nw[:, 2, :], nw[:, 1, :], -0.5, 1.5, ALU.mult, ALU.add).then_inc(newton, 1)
                    gp.wait_ge(newton, k + (4 * n + 3))
                    gp.tensor_tensor(rstd[:, n + 1, :], nw[:, 2, :], r, ALU.mult).then_inc(newton, 1)
                gp.wait_ge(newton, k + 4 * NEWTON)
                if half == 0:
                    gp.wait_ge(wsum_made, s)
                C = HALF // COLG
                at = half * C * UNITS
                adj_v = adjt[:, ds(s, 1), :].rearrange("p o (q r) -> p (o q) r", q=COLG)[:, :, at:at + C * UNITS]
                w_v = wn[:, :].rearrange("p (q r) -> p q r", q=COLG)[:, :, at:at + C * UNITS]
                gp.tensor_tensor(w_v.rearrange("p q (c e) -> p q c e", e=UNITS), adj_v.rearrange("p q (c e) -> p q c e", e=UNITS),
                                 rstd[:, NEWTON, :].rearrange("p (c q e) -> p q c e", q=COLG, e=UNITS), ALU.mult).then_inc(wn_ready, 1)
                wait_apart(gp, wn_ready, count)
                z_v = z[:, ZW * half * HALF:ZW * (half + 1) * HALF].rearrange("p (c q r) -> p c q r", q=COLG, r=ZW)[:, :, :, ZP:ZW]
                gp.tensor_copy(z_v, w_v.rearrange("p q (c e) -> p c q e", e=UNITS)).then_inc(w_ready, 1)

            def scale_b2(s):
                gp.wait_ge(wsum_moved, s + 1)
                gp.tensor_tensor(sb2[:, :], b2c[:, :], wsum[:, :].broadcast_to([N, HID]), ALU.mult).then_inc(sb2_ready, 1)

            def combine(s):
                gp.tensor_tensor(ep[:, 0, :], betar[:, :], rsum[:, ds(s, 1)].broadcast_to([N, HID]), ALU.mult).then_inc(ep_beta, 1)
                gp.wait_ge(contr_free, s + 1)
                gp.tensor_tensor(ep[:, 1, :], acc[:, UNITS - 1, :], gammar[:, :], ALU.mult).then_inc(ep_gamma, 1)
                gp.wait_ge(ep_gamma, s + 1)
                gp.wait_ge(ep_beta, s + 1)
                gp.wait_ge(x1_kept, s + 1)
                gp.tensor_tensor(ep[:, 2:3, :], ep[:, 1:2, :], nodes[:, ds(s, 1), :], ALU.add).then_inc(ep_x1, 1)
                gp.wait_ge(ep_x1, s + 1)
                gp.tensor_tensor(ep[:, 3, :], ep[:, 2, :], ep[:, 0, :], ALU.add).then_inc(ep_sum, 1)

            def finish(s):
                wait_apart(gp, ep_aggr, s + 1)
                gp.tensor_scalar(eprs[:, 0:1], epmv[:, 1:2], EPS, None, ALU.add).then_inc(ep_var, 1)
                gp.wait_ge(ep_var, s + 1)
                gp.tensor_tensor(eprs[:, 1:2], eprs[:, 0:1], neghalf[:, :], ALU.pow).then_inc(ep_rstd, 1)
                gp.tensor_tensor(ep[:, 2, :], ep[:, 3, :], epmv[:, 0:1].broadcast_to([N, HID]), ALU.subtract).then_inc(ep_centred, 1)
                gp.wait_ge(ep_rstd, s + 1)
                gp.wait_ge(ep_centred, s + 1)
                gp.tensor_tensor(adjn[:, ds(s, 1), :], ep[:, 2:3, :], eprs[:, 1:2].unsqueeze(1).broadcast_to([N, 1, HID]), ALU.mult).then_inc(ep_done, 1)

            gp.wait_ge(consts_l0, N_CONST_L0)
            degree(1)
            gp.memset(a[:, BLANKS[3]:BLANKS[4], :], 0.0).then_inc(blank, 1)
            normalise(1)
            keep_x1(1)
            gp.wait_ge(w2s, 5)
            with gp.Fori(1, BATCH + 1) as s:
                gather_var(s - 1, 1, s * 2, s * GROUPS)
                degree(s + 1)
                weights(s - 1, 1, s * 2)
                normalise(s + 1)
                scale_b2(s - 1)
                gather_var(s, 0, s * 2 + 1, s * GROUPS + HALF)
                keep_x1(s + 1)
                weights(s, 0, s * 2 + 1)
                combine(s - 1)
                finish(s - 1)
            gather_var(BATCH, 1, (BATCH + 1) * 2, (BATCH + 1) * GROUPS)
            weights(BATCH, 1, (BATCH + 1) * 2)
            scale_b2(BATCH)
            combine(BATCH)
            finish(BATCH)

        @block.vector
        def _(ve):
            def half_units(g):
                late = int(g >= EARLY)
                for e in range(VUNITS):
                    i = node(g, e)
                    last = ve.tensor_scalar(h[:, g % HRING, e, :], uv[:, late, 1, :], uv[:, late, 0, i:i + 1], 0.0, ALU.add, ALU.max)
                last.then_inc(h_dve, 1)

            def take_stats(g, count):
                ve.wait_ge(a_moved, count)
                for pr in range(2):
                    last = ve.bn_stats(st[:, UNITS * g + 2 * pr:UNITS * g + 2 * pr + 2, :].rearrange("p e c -> p (e c)"),
                                       a[:, g, 2 * pr * WX:2 * pr * WX + 2 * HID])
                last.then_inc(a_stat, 1)

            def row_sums(s):
                ve.wait_ge(loaded, (s + 1) * 48)
                ve.reduce_sum(rsum[:, ds(s, 1)], adjn[:, ds(s, 1), :], mybir.AxisListType.X).then_inc(rsum_ready, 1)

            def residual(s, part):
                if part == 0:
                    ve.wait_ge(lin_made, s)
                    ve.scalar_tensor_tensor(l0[:, 0, :], misc[:, 1, :], deg[:, 1:2], b0r[:, :], ALU.mult, ALU.add).then_inc(lin_scaled, 1)
                elif part == 1:
                    ve.wait_ge(lin_scaled, s)
                    ve.scalar_tensor_tensor(l0[:, 1:2, :], l0[:, 0:1, :], 0.0, nodes[:, ds(s, 1), :], ALU.max, ALU.add).then_inc(res_ready, 1)
                elif part == 2:
                    ve.wait_ge(res_ready, s)
                    ve.bn_stats(l0st[:, :], l0[:, 1, :]).then_inc(l0_stats, 1)
                else:
                    wait_apart(ve, l0_stats, s)
                    ve.bn_aggr(l0mv[:, :], l0st[:, :]).then_inc(l0_aggr, 1)

            def seed(count):
                ve.wait_ge(var_ready, count)
                ve.tensor_scalar(rstd[:, 0, :].bitcast(int32), var[:, :].bitcast(int32), -0.5, float(SEED), ALU.mult, ALU.add).then_inc(seeded, 1)

            def pick(s, m):
                if m == 0:
                    ve.wait_ge(contracted, s * STEPS + STEPS)
                    ve.wait_ge(sb2_ready, s + 1)
                else:
                    ve.wait_ge(picking, s * 3 + m)
                prev = sb2[:, :] if m == 0 else acc[:, m - 1, :]
                ve.scalar_tensor_tensor(acc[:, m, :], contr[:, m, :], diag4[:, m:m + 1], prev, ALU.mult, ALU.add)\
                  .then_inc(picking if m < UNITS - 1 else contr_free, 1)

            def end_stats(s, part):
                if part == 0:
                    ve.wait_ge(ep_sum, s + 1)
                    ve.bn_stats(epst[:, :], ep[:, 3, :]).then_inc(ep_stats, 1)
                else:
                    wait_apart(ve, ep_stats, s + 1)
                    ve.bn_aggr(epmv[:, :], epst[:, :]).then_inc(ep_aggr, 1)

            ve.memset(st[:, :, :], 0.0).then_inc(filled, 1)
            ve.memset(a[:, BLANKS[0]:BLANKS[1], :], 0.0).then_inc(blank_first, 1)
            ve.sem_inc(a_stat, GROUPS - 1)
            ve.sem_inc(h_dve, GROUPS)
            ve.sem_inc(seeded, 1)
            ve.wait_ge(filled, N_FILLED)
            row_sums(1)
            ve.wait_ge(consts, N_CONST)
            ve.reduce_sum(sums[:, 0:1], w2raw[:, :], mybir.AxisListType.X).then_inc(w2s, 1)
            ve.reduce_sum(sums[:, 1:2], b2raw[:, :], mybir.AxisListType.X).then_inc(b2s, 1)
            ve.wait_ge(w2s, 1)
            ve.wait_ge(b2s, 1)
            ve.tensor_scalar(sums[:, 0:2], sums[:, 0:2], -1.0 / HID, None, ALU.mult).then_inc(w2s, 1)
            ve.wait_ge(w2s, 2)
            ve.tensor_scalar(w2x[:, 0:HID], w2raw[:, :], sums[:, 0:1], None, ALU.add).then_inc(w2s, 1)
            ve.tensor_scalar(b2c[:, :], b2raw[:, :], sums[:, 1:2], None, ALU.add).then_inc(b2s, 1)
            ve.wait_ge(w2s, 3)
            ve.wait_ge(b2s, 2)
            ve.scalar_tensor_tensor(junk[:, :], w2x[:, 0:HID], 2.0, b2c[:, :], ALU.mult, ALU.mult,
                                    accum_out=w2x[:, HID:WX]).then_inc(w2s, 1)
            ve.wait_ge(w2s, 4)
            ve.scalar_tensor_tensor(junk[:, :], b2c[:, :], 1.0, b2c[:, :], ALU.mult, ALU.mult,
                                    accum_out=sums[:, 2:3]).then_inc(b2s, 1)
            ve.wait_ge(b2s, 3)
            ve.tensor_scalar(sums[:, 3:4], sums[:, 2:3], 1.0 / HID, EPS, ALU.mult, ALU.add).then_inc(w2s, 1)

            ve.memset(a[:, BLANKS[2]:BLANKS[3], :], 0.0).then_inc(blank, 1)
            ve.wait_ge(consts_l0, N_CONST_L0)
            for part in range(4):
                residual(1, part)
            ve.wait_ge(uv_moved, 1)
            for g in range(LEAD):
                half_units(g)
            with ve.Fori(1, BATCH + 1) as s:
                base = ve.snap(s * GROUPS)
                for g in range(GROUPS):
                    ahead = (g + LEAD) % GROUPS
                    if g + LEAD == GROUPS:
                        ve.wait_ge(uv_moved, s + 1)
                    if ahead == EARLY:
                        ve.wait_ge(uv_late, s)
                    if g == 0:
                        row_sums(s + 1)
                    if g == 4:
                        seed(s * 2)
                    if 13 <= g < 17:
                        residual(s + 1, g - 13)
                    if g == 20:
                        seed(s * 2 + 1)
                    if g == 25:
                        pick(s - 1, 2)
                    if g in (29, 31):
                        end_stats(s - 1, (g - 29) // 2)
                    half_units(ahead)
                    if g == 24:
                        pick(s - 1, 0)
                    if g == 25:
                        pick(s - 1, 3)
                    take_stats((g - 1) % GROUPS, base + g)
                    if g == 24:
                        pick(s - 1, 1)
            take_stats(GROUPS - 1, (BATCH + 1) * GROUPS)
            seed((BATCH + 1) * 2)
            for m in range(UNITS):
                pick(BATCH, m)
            for part in range(2):
                end_stats(BATCH, part)

        @block.scalar
        def _(ac):
            def half_units(g):
                late = int(g >= EARLY)
                for e in range(VUNITS, UNITS):
                    i = node(g, e)
                    last = ac.activation(h[:, g % HRING, e, :], uv[:, late, 1, :], ACT.Relu, bias=uv[:, late, 0, i:i + 1])
                last.then_inc(h_act, 1)

            def move_a(g, base, s):
                if g % COLG == 0:
                    ac.wait_ge(contracted, (s - 1) * STEPS + (g // COLG + 1))
                ac.wait_ge(a_made, base + (g + 1))
                ac.activation(a[:, g, :].rearrange("p (b w e) -> p b e w", b=2, e=2),
                              ring[:, g % PRING, :, 0:2 * WX].rearrange("p b (e w) -> p b e w", e=2), ACT.Copy).then_inc(a_moved, 1)

            def move_uv(s, copy):
                ac.wait_ge(uv_made, s)
                ac.activation(uv[:, copy, 0, :], misc[:, 0, :], ACT.Identity, bias=b1c[:, :]).then_inc(u_moved, 1)
                ac.activation(uv[:, copy, 1, :], misc[:, 1, :], ACT.Copy).then_inc(uv_late if copy else uv_moved, 1)

            def move_supp(s):
                ac.wait_ge(supp_made, s)
                ac.activation(supp_t[:, :], misc[:, 0, :], ACT.Copy).then_inc(supp_moved, 1)

            def move_x1t(s):
                ac.wait_ge(x1t_made, s)
                ac.activation(x1t[:, :], misc[:, 2, :], ACT.Copy).then_inc(x1t_moved, 1)

            def move_wsum(s):
                ac.wait_ge(wsum_made, s + 1)
                ac.activation(wsum[:, :], misc[:, 3, 0:1], ACT.Copy).then_inc(wsum_moved, 1)

            for dst, src in ((ident[:, :], ident_in), (w0t[:, :], w0_t),
                             (b0r[:, :], b0.unsqueeze(0).broadcast_to([N, F])),
                             (w1a[:, :], w1[0:F, :]), (w1b[:, :], w1[F:2 * F, :]), (b1c[:, :], b1.unsqueeze(1))):
                ac.dma_start(dst, src).then_inc(consts_l0, 16)
            ac.sem_inc(a_moved, GROUPS)
            ac.sem_inc(h_act, GROUPS)
            ac.wait_ge(consts_l0, N_CONST_L0)
            ac.wait_ge(filled, N_FILLED)
            move_supp(1)
            ac.wait_ge(blank_first, 1)
            ac.wait_ge(blank, 3)
            move_x1t(1)
            move_uv(1, 0)
            move_uv(1, 1)
            ac.wait_ge(u_moved, 2)
            ac.wait_ge(uv_moved, 1)
            for g in range(LEAD):
                half_units(g)
            with ac.Fori(1, BATCH + 1) as s:
                base = ac.snap(s * GROUPS)
                for g in range(GROUPS):
                    ahead = (g + LEAD) % GROUPS
                    if ahead == 0:
                        ac.wait_ge(u_moved, s * 2 + 1)
                        ac.wait_ge(uv_moved, s + 1)
                    if ahead == EARLY:
                        ac.wait_ge(u_moved, s * 2)
                        ac.wait_ge(uv_late, s)
                    half_units(ahead)
                    if g == 10:
                        move_supp(s + 1)
                    if g == 16:
                        move_wsum(s - 1)
                    if g == 21:
                        move_x1t(s + 1)
                    if g == 24:
                        ac.wait_ge(h_dve, base + EARLY)
                        ac.wait_ge(h_act, base + EARLY)
                        move_uv(s + 1, 0)
                    if g == GROUPS - LEAD + 2:
                        ac.wait_ge(h_dve, base + GROUPS)
                        ac.wait_ge(h_act, base + GROUPS)
                        move_uv(s + 1, 1)
                    move_a(g, base, s)
            move_wsum(BATCH)

        @block.tensor
        def _(pe):
            def products(g, base):
                pe.wait_ge(h_dve, base + (g + 1))
                pe.wait_ge(h_act, base + (g + 1))
                if g < 2:
                    pe.wait_ge(a_moved, base - (1 - g))
                elif g >= PRING:
                    pe.wait_ge(a_moved, base + (g - PRING + 1))
                for e in range(UNITS):
                    last = pe.matmul(ring[:, g % PRING, e // 2, WX * (e % 2):WX * (e % 2 + 1)], h[:, g % HRING, e, :], w2x[:, :],
                                     start=True, stop=True)
                last.then_inc(a_made, 1)

            def contract(step, s):
                if step == 0 and not isinstance(s, int):
                    pe.wait_ge(contr_free, s)
                if step % (STEPS // 2) == 0 or step == 2:
                    pe.wait_ge(w_ready, s * 2 + (1 + step // (STEPS // 2)))
                for q in range(COLG):
                    g = COLG * step + q
                    at = ZP + ZW * g - UNITS * step
                    last = pe.matmul(contr[32 * q:32 * q + 32, :, :], z[:, at:at + ZW],
                                     a[:, g, :].rearrange("p (b w e) -> p b e w", b=2, e=2)[:, :, :, 0:HID],
                                     start=(step == 0), stop=(step == STEPS - 1))
                last.then_inc(contracted, 1)

            def sum_w(s):
                pe.wait_ge(w_ready, s * 2 + 2)
                pe.matmul(misc[:, 3, 0:1], wn[:, :], ones[:, :], start=True, stop=True).then_inc(wsum_made, 1)

            def support(s):
                pe.wait_ge(xs_ready, s)
                pe.wait_ge(ahat_ready, s)
                if not isinstance(s, int):
                    pe.wait_ge(uv_late, s - 1)
                pe.matmul(misc[:, 0, :], xs[:, :], ahat_t[:, :], start=True, stop=True).then_inc(supp_made, 1)

            def linear(s):
                pe.wait_ge(supp_moved, s)
                pe.matmul(misc[:, 1, :], supp_t[:, :], w0t[:, :], start=True, stop=True).then_inc(lin_made, 1)

            def transpose_x1(s):
                pe.wait_ge(x1_ready, s)
                pe.transpose(misc[:, 2, :], x1s[:, :], ident[:, :]).then_inc(x1t_made, 1)

            def project(s):
                pe.wait_ge(x1t_moved, s)
                pe.matmul(misc[:, 0, :], w1a[:, :], x1t[:, :], start=True, stop=True)
                pe.matmul(misc[:, 1, :], w1b[:, :], x1t[:, :], start=True, stop=True).then_inc(uv_made, 1)

            pe.sem_inc(a_made, GROUPS)
            pe.wait_ge(filled, N_FILLED)
            pe.wait_ge(blank_first, 1)
            contract(0, 0)
            contract(1, 0)
            pe.wait_ge(consts_l0, N_CONST_L0)
            support(1)
            linear(1)
            transpose_x1(1)
            project(1)
            pe.wait_ge(blank, 3)
            pe.wait_ge(w2s, 5)
            with pe.Fori(1, BATCH + 1) as s:
                base = pe.snap(s * GROUPS)
                for g in range(GROUPS):
                    products(g, base)
                    if g % COLG == COLG - 1:
                        step, before = step_at(g)
                        contract(step, s - 1 if before else s)
                    if g == 9:
                        support(s + 1)
                    if g == 12:
                        linear(s + 1)
                    if g == 15:
                        pe.wait_ge(lin_scaled, s + 1)
                        sum_w(s - 1)
                    if g == 20:
                        pe.wait_ge(wsum_moved, s)
                        transpose_x1(s + 1)
                    if g == 22:
                        project(s + 1)
            for step in range(2, STEPS):
                contract(step, BATCH)
                if step == STEPS // 2:
                    pe.wait_ge(uv_late, BATCH + 1)
                    sum_w(BATCH)


def kernel(x, adj, L0_gnn_W, L0_gnn_b, L1_gnn_W1, L1_gnn_b1, L1_gnn_W2, L1_gnn_b2, L1_gnn_gamma, L1_gnn_beta):
    import numpy as np
    import concourse.bacc as bacc
    from concourse.bass_utils import run_bass_kernel_spmd

    arrays = {
        "x": x, "adj": adj,
        "adj_t": np.transpose(np.asarray(adj), (0, 2, 1)),
        "w0_t": np.transpose(np.asarray(L0_gnn_W)),
        "b0": L0_gnn_b, "w1": L1_gnn_W1, "b1": L1_gnn_b1, "w2": L1_gnn_W2, "b2": L1_gnn_b2,
        "gamma": L1_gnn_gamma, "beta": L1_gnn_beta,
        "ident": np.eye(128, dtype=np.float32),
        "diag4": np.tile(np.eye(4, dtype=np.float32), (32, 1)),
    }
    arrays = {n: np.ascontiguousarray(v) for n, v in arrays.items()}
    nc = bacc.Bacc("TRN2", target_bir_lowering=False, num_devices=1)
    args = [nc.dram_tensor("in_" + n, v.shape, mybir.dt.from_np(v.dtype), kind="ExternalInput").ap() for n, v in arrays.items()]
    args.append(nc.dram_tensor("out", (64, 128, 128), mybir.dt.float32, kind="ExternalOutput").ap())
    gnn_two_layer_kernel(nc, *args)
    r = run_bass_kernel_spmd(nc, [{"in_" + n: v for n, v in arrays.items()}], core_ids=[0])
    return r.results[0]["out"]
```
